# Optimizing a Trainium2 kernel written in Bass

```python
import numpy as np
import jax
import jax.numpy as jnp

def _softmax(x, axis=-1):
    return jax.nn.softmax(x, axis=axis)

def _gelu(x):
    return jax.nn.gelu(x, approximate=True)

def _silu(x):
    return jax.nn.silu(x)

def _sigmoid(x):
    return jax.nn.sigmoid(x)

def _layernorm(x, axis=-1, eps=1e-05):
    m = jnp.mean(x, axis=axis, keepdims=True)
    v = jnp.var(x, axis=axis, keepdims=True)
    return (x - m) / jnp.sqrt(v + eps)

def _scatter_add(tgt, idx, src, axis=0):
    return tgt.at[idx].add(src)

def _segment_sum(src, seg, n):
    return jax.ops.segment_sum(src, seg, n)
kernel_name = 'mk_macaron_d1_jaxref_r8_57b42b'

def setup_inputs(seed: int=0):
    np.random.seed(seed)
    _w = jnp.asarray

    def _L0_attn_setup():
        import jax, jax.numpy as jnp
        import numpy as np
        B, T, C, H, VBD = (2, 256, 128, 16, 256)
        KD = C // H
        VD = VBD // H
        EPS = float(np.finfo(np.float32).eps)

        def _inner_mask(seq_len):
            gamma = jnp.log(1.0 - 2.0 ** (-5.0 - jnp.arange(H, dtype=jnp.float32)))
            idx = jnp.arange(seq_len, dtype=jnp.float32)
            diff = idx[:, None] - idx[None, :]
            causal = diff >= 0
            decay = jnp.where(causal, jnp.exp(gamma[:, None, None] * diff), 0.0)
            scale = jnp.sqrt(decay.sum(-1, keepdims=True))
            return decay / scale
        key = jax.random.key(seed)
        ks = jax.random.split(key, 9)
        s = 0.02
        return {'x': jax.random.normal(ks[0], (B, T, C), dtype=jnp.float32), 'W_qk': jax.random.normal(ks[1], (C, 2 * C), dtype=jnp.float32) * s, 'b_qk': jnp.zeros((2 * C,), dtype=jnp.float32), 'W_v': jax.random.normal(ks[2], (C, VBD), dtype=jnp.float32) * s, 'b_v': jnp.zeros((VBD,), dtype=jnp.float32), 'W_g': jax.random.normal(ks[3], (C, VBD), dtype=jnp.float32) * s, 'b_g': jnp.zeros((VBD,), dtype=jnp.float32), 'W_o': jax.random.normal(ks[4], (VBD, C), dtype=jnp.float32) * s, 'b_o': jnp.zeros((C,), dtype=jnp.float32)}
    _L0_attn_in = _L0_attn_setup()

    def _L0_ffn_setup():
        import jax, jax.numpy as jnp
        import numpy as np
        import math
        N_EMBD = 128
        HIDDEN = 4 * N_EMBD
        N_EXPERTS = 8
        TOP_K = 2
        B, T = (4, 256)

        def new_gelu(x):
            c = math.sqrt(2.0 / math.pi)
            return 0.5 * x * (1.0 + jnp.tanh(c * (x + 0.044715 * x * x * x)))

        def _moe_forward(x, Wfc_s, bfc_s, Wproj_s, bproj_s, Wr, Wfc, bfc, Wproj, bproj):
            Bb, Tt, C = x.shape
            xf = x.reshape(Bb * Tt, C)
            N = Bb * Tt
            shared = new_gelu(xf @ Wfc_s + bfc_s) @ Wproj_s + bproj_s
            logits = xf @ Wr
            probs = jax.nn.softmax(logits, axis=-1)
            topk_p, topk_i = jax.lax.top_k(probs, TOP_K)
            topk_p = topk_p / jnp.sum(topk_p, axis=-1, keepdims=True)
            gate = jnp.zeros((N, N_EXPERTS), dtype=xf.dtype)
            gate = gate.at[jnp.arange(N)[:, None], topk_i].add(topk_p)
            routed = jnp.zeros_like(xf)
            for e in range(N_EXPERTS):
                h = new_gelu(xf @ Wfc[e] + bfc[e]) @ Wproj[e] + bproj[e]
                routed = routed + h * gate[:, e:e + 1]
            return (shared + routed).reshape(Bb, Tt, C)
        key = jax.random.key(seed)
        ks = jax.random.split(key, 10)
        s = 0.02
        return {'x': jax.random.normal(ks[0], (B, T, N_EMBD), dtype=jnp.float32), 'Wfc_s': jax.random.normal(ks[1], (N_EMBD, HIDDEN), dtype=jnp.float32) * s, 'bfc_s': jnp.zeros((HIDDEN,), dtype=jnp.float32), 'Wproj_s': jax.random.normal(ks[2], (HIDDEN, N_EMBD), dtype=jnp.float32) * s, 'bproj_s': jnp.zeros((N_EMBD,), dtype=jnp.float32), 'Wr': jax.random.normal(ks[3], (N_EMBD, N_EXPERTS), dtype=jnp.float32) * s, 'Wfc': jax.random.normal(ks[4], (N_EXPERTS, N_EMBD, HIDDEN), dtype=jnp.float32) * s, 'bfc': jnp.zeros((N_EXPERTS, HIDDEN), dtype=jnp.float32), 'Wproj': jax.random.normal(ks[5], (N_EXPERTS, HIDDEN, N_EMBD), dtype=jnp.float32) * s, 'bproj': jnp.zeros((N_EXPERTS, N_EMBD), dtype=jnp.float32)}
    _L0_ffn_in = _L0_ffn_setup()
    _d = {'L0_attn_x': _L0_attn_in['x'], 'L0_attn_W_qk': _L0_attn_in['W_qk'], 'L0_attn_b_qk': _L0_attn_in['b_qk'], 'L0_attn_W_v': _L0_attn_in['W_v'], 'L0_attn_b_v': _L0_attn_in['b_v'], 'L0_attn_W_g': _L0_attn_in['W_g'], 'L0_attn_b_g': _L0_attn_in['b_g'], 'L0_attn_W_o': _L0_attn_in['W_o'], 'L0_attn_b_o': _L0_attn_in['b_o'], 'L0_ffn_Wfc_s': _L0_ffn_in['Wfc_s'], 'L0_ffn_bfc_s': _L0_ffn_in['bfc_s'], 'L0_ffn_Wproj_s': _L0_ffn_in['Wproj_s'], 'L0_ffn_bproj_s': _L0_ffn_in['bproj_s'], 'L0_ffn_Wr': _L0_ffn_in['Wr'], 'L0_ffn_Wfc': _L0_ffn_in['Wfc'], 'L0_ffn_bfc': _L0_ffn_in['bfc'], 'L0_ffn_Wproj': _L0_ffn_in['Wproj'], 'L0_ffn_bproj': _L0_ffn_in['bproj']}
    _x0 = _d['L0_attn_x']
    _d['L0_attn_x'] = jax.random.normal(jax.random.fold_in(jax.random.key(seed), 1), (32, 256, 128), dtype=_x0.dtype)
    del _x0
    return _d

def reference(L0_attn_x, L0_attn_W_qk, L0_attn_b_qk, L0_attn_W_v, L0_attn_b_v, L0_attn_W_g, L0_attn_b_g, L0_attn_W_o, L0_attn_b_o, L0_ffn_Wfc_s, L0_ffn_bfc_s, L0_ffn_Wproj_s, L0_ffn_bproj_s, L0_ffn_Wr, L0_ffn_Wfc, L0_ffn_bfc, L0_ffn_Wproj, L0_ffn_bproj):

    def _L0_attn_ref(x, W_qk, b_qk, W_v, b_v, W_g, b_g, W_o, b_o):
        import jax, jax.numpy as jnp
        import numpy as np
        B, T, C, H, VBD = (2, 256, 128, 16, 256)
        KD = C // H
        VD = VBD // H
        EPS = float(np.finfo(np.float32).eps)

        def _inner_mask(seq_len):
            gamma = jnp.log(1.0 - 2.0 ** (-5.0 - jnp.arange(H, dtype=jnp.float32)))
            idx = jnp.arange(seq_len, dtype=jnp.float32)
            diff = idx[:, None] - idx[None, :]
            causal = diff >= 0
            decay = jnp.where(causal, jnp.exp(gamma[:, None, None] * diff), 0.0)
            scale = jnp.sqrt(decay.sum(-1, keepdims=True))
            return decay / scale
        Bx, Tx, _ = x.shape
        qk = x @ W_qk + b_qk
        q, k = jnp.split(qk, 2, axis=-1)
        v = x @ W_v + b_v
        q = q.reshape(Bx, Tx, H, KD).transpose(0, 2, 1, 3)
        k = k.reshape(Bx, Tx, H, KD).transpose(0, 2, 1, 3)
        v = v.reshape(Bx, Tx, H, VD).transpose(0, 2, 1, 3)
        mask = _inner_mask(Tx)
        scores = jnp.einsum('bhtd,bhsd->bhts', q, k) * mask
        denom = jnp.clip(jnp.abs(scores).sum(-1, keepdims=True), 1.0, 50000.0)
        scores = scores / denom
        ret = jnp.einsum('bhts,bhsv->bthv', scores, v)
        ret = ret * jax.lax.rsqrt(jnp.mean(ret * ret, axis=-1, keepdims=True) + EPS)
        y = ret.reshape(Bx, Tx, H * VD)
        gated = (x @ W_g + b_g) * y
        return gated @ W_o + b_o

    def _L0_ffn_ref(x, Wfc_s, bfc_s, Wproj_s, bproj_s, Wr, Wfc, bfc, Wproj, bproj):
        import jax, jax.numpy as jnp
        import numpy as np
        import math
        N_EMBD = 128
        HIDDEN = 4 * N_EMBD
        N_EXPERTS = 8
        TOP_K = 2
        B, T = (4, 256)

        def new_gelu(x):
            c = math.sqrt(2.0 / math.pi)
            return 0.5 * x * (1.0 + jnp.tanh(c * (x + 0.044715 * x * x * x)))

        def _moe_forward(x, Wfc_s, bfc_s, Wproj_s, bproj_s, Wr, Wfc, bfc, Wproj, bproj):
            Bb, Tt, C = x.shape
            xf = x.reshape(Bb * Tt, C)
            N = Bb * Tt
            shared = new_gelu(xf @ Wfc_s + bfc_s) @ Wproj_s + bproj_s
            logits = xf @ Wr
            probs = jax.nn.softmax(logits, axis=-1)
            topk_p, topk_i = jax.lax.top_k(probs, TOP_K)
            topk_p = topk_p / jnp.sum(topk_p, axis=-1, keepdims=True)
            gate = jnp.zeros((N, N_EXPERTS), dtype=xf.dtype)
            gate = gate.at[jnp.arange(N)[:, None], topk_i].add(topk_p)
            routed = jnp.zeros_like(xf)
            for e in range(N_EXPERTS):
                h = new_gelu(xf @ Wfc[e] + bfc[e]) @ Wproj[e] + bproj[e]
                routed = routed + h * gate[:, e:e + 1]
            return (shared + routed).reshape(Bb, Tt, C)
        return _moe_forward(x, Wfc_s, bfc_s, Wproj_s, bproj_s, Wr, Wfc, bfc, Wproj, bproj)
    x = L0_attn_x
    x = x + 0.5 * _L0_ffn_ref(_layernorm(x, axis=-1), L0_ffn_Wfc_s, L0_ffn_bfc_s, L0_ffn_Wproj_s, L0_ffn_bproj_s, L0_ffn_Wr, L0_ffn_Wfc, L0_ffn_bfc, L0_ffn_Wproj, L0_ffn_bproj)
    x = x + _L0_attn_ref(_layernorm(x, axis=-1), L0_attn_W_qk, L0_attn_b_qk, L0_attn_W_v, L0_attn_b_v, L0_attn_W_g, L0_attn_b_g, L0_attn_W_o, L0_attn_b_o)
    x = x + 0.5 * _L0_ffn_ref(_layernorm(x, axis=-1), L0_ffn_Wfc_s, L0_ffn_bfc_s, L0_ffn_Wproj_s, L0_ffn_bproj_s, L0_ffn_Wr, L0_ffn_Wfc, L0_ffn_bfc, L0_ffn_Wproj, L0_ffn_bproj)
    return x

_drawn_inputs = setup_inputs


def setup_inputs(seed=0):
    import zlib

    import numpy as np

    out = dict(_drawn_inputs(seed))
    spreads = {'L0_attn_b_qk': (0.0, 0.1),
     'L0_attn_b_v': (0.0, 0.1),
     'L0_attn_b_g': (0.0, 0.1),
     'L0_attn_b_o': (0.0, 0.1),
     'L0_ffn_bfc_s': (0.0, 0.301),
     'L0_ffn_bproj_s': (0.0, 0.1),
     'L0_ffn_bfc': (0.0, 0.48),
     'L0_ffn_bproj': (0.0, 0.1)}
    factors = {}
    for name, (base, spread) in spreads.items():
        noise = np.random.default_rng([zlib.crc32(name.encode()), seed]).standard_normal(out[name].shape)
        drawn = base * np.exp(spread * noise) if base else spread * noise
        out[name] = jnp.asarray(drawn.astype(out[name].dtype))
    for name, factor in factors.items():
        out[name] = (out[name] * factor).astype(out[name].dtype)
    return out
```

```python
from contextlib import ExitStack

import numpy as np
import concourse.bass as bass
from concourse import mybir

F32 = mybir.dt.float32
F32R = mybir.dt.float32r
U32 = mybir.dt.uint32
ALU = mybir.AluOpType
ACT = mybir.ActivationFunctionType
AX = mybir.AxisListType
ds = bass.ds

P = 128
SEQ = 256
HEADS, KD, VD = 16, 8, 16
VB = HEADS * VD
HID = 512
NE = 8
EX = NE + 1
TOK = 512
SUB = TOK // P
CH = HID // P
LN_EPS = 1e-5
RMS_EPS = float(np.finfo(np.float32).eps)
DENOM_LO, DENOM_HI = 1.0, 50000.0
H_RING, HL_RING, UP_RING, Y_RING, T_RING = 3, 6, 3, 3, 2
CAUSAL = 3 * P
C_ID, C_IOTA, C_QLOW, C_KLOW, C_END = 0, P, P + NE, P + NE + 1, P + NE + 2


def ffn_phase(nc, m, name, load, store):
    tiles = m["tokens"] // TOK
    ctx = ExitStack()
    with ctx:
        def sb(n, shape, dt=F32):
            return ctx.enter_context(nc.sbuf_tensor(f"{name}_{n}", shape, dt))

        def pb(n):
            return ctx.enter_context(nc.psum_tensor(f"{name}_{n}", [P, 512], F32))

        def sem(n):
            return ctx.enter_context(nc.semaphore(f"{name}_{n}"))

        x, w_hi, w_lo, const = m["x"], m["w_hi"], m["w_lo"], m["const"]
        wr, b_up, b_down = m["wr"], m["b_up"], m["b_down"]
        ident = const[:, C_ID:C_ID + P]
        h = [sb(f"h{i}", [P, 2 * TOK]) for i in range(H_RING)]
        h_hi = [sb(f"h_hi{i}", [P, 2 * TOK], F32R) for i in range(HL_RING)]
        h_lo = [sb(f"h_lo{i}", [P, 2 * TOK], F32R) for i in range(HL_RING)]
        gate_bc = sb("gate_bc", [P, NE, TOK])
        xn = sb("xn", [P, SUB, P])
        xf = sb("xf", [P, TOK])
        x_hi = sb("x_hi", [P, TOK], F32R)
        x_lo = sb("x_lo", [P, TOK], F32R)
        acc = sb("acc", [P, TOK])
        gated = [sb(f"gated{i}", [P, TOK]) for i in range(T_RING)]
        gate_t = sb("gate_t", [EX, TOK])
        stats = sb("stats", [P, SUB, 6])
        mv = sb("mv", [P, SUB, 2])
        veps = sb("veps", [P, SUB])
        rstd = sb("rstd", [P, SUB])
        eps = sb("eps", [P, SUB])
        carrier = sb("carrier", [P, 1])
        half_neg = sb("half_neg", [P, SUB])
        euler = sb("euler", [P, SUB])
        logits = sb("logits", [P, SUB, NE])
        top = sb("top", [P, SUB, 8])
        topi = sb("topi", [P, SUB, 8], U32)
        gap = sb("gap", [P, SUB])
        egap = sb("egap", [P, SUB])
        egap1 = sb("egap1", [P, SUB])
        g1 = sb("g1", [P, SUB])
        g2 = sb("g2", [P, SUB])
        eq1 = sb("eq1", [P, SUB, NE])
        eq2 = sb("eq2", [P, SUB, NE])
        gate = sb("gate", [P, SUB, EX])
        stage = [sb(f"stage{i}", [P, 2 * HID]) for i in range(2)] if load else None

        up_ps = [pb(f"up{i}") for i in range(UP_RING)]
        y_ps = [pb(f"y{i}") for i in range(Y_RING)]
        t_ps = pb("t")
        r_ps = pb("r")

        loaded_x0, loaded_x1, loaded_x = sem("loaded_x0"), sem("loaded_x1"), sem("loaded_x")
        loaded_small = sem("loaded_small")
        loaded_w = [sem(f"loaded_w{e}") for e in range(EX)] if load else None
        w_hi_done, w_lo_done = sem("w_hi_done"), sem("w_lo_done")
        stored = sem("stored")
        preset = sem("preset")
        up_done, gelu_done, hi_done, lo_done = sem("up_done"), sem("gelu_done"), sem("hi_done"), sem("lo_done")
        down_done, y_taken, acc_added = sem("down_done"), sem("y_taken"), sem("acc_added")
        acc_turned, x_updated = sem("acc_turned"), sem("x_updated")
        stats_step, var_eps, rstd_done, xn_done = sem("stats_step"), sem("var_eps"), sem("rstd_done"), sem("xn_done")
        xn_turned, xf_done, xs_hi, xs_done = sem("xn_turned"), sem("xf_done"), sem("xs_hi"), sem("xs_done")
        logits_done, router_step, egap_done = sem("logits_done"), sem("router_step"), sem("egap_done")
        gate_turned, gate_t_done = sem("gate_turned"), sem("gate_t_done")
        gates_out, gates_a, gates_b = sem("gates_out"), sem("gates_b1"), sem("gates_b2")
        STATS = 2 * SUB
        ROUTER = 7 + 2 * SUB
        block = ctx.enter_context(nc.Block())

        def first(t):
            return isinstance(t, int) and t == 0

        @block.sync
        def _(sp):
            def spread_gates(t):
                sp.wait_ge(gate_t_done, t + 1)
                if not first(t):
                    sp.wait_ge(gates_a, 16 * t)
                    sp.wait_ge(gates_b, 16 * t)
                sp.dma_start(m["gate_dram"], gate_t[0:NE, :]).then_inc(gates_out, 16)
                sp.wait_ge(gates_out, 16 * (t + 1))
                half = NE // 2
                if not first(t):
                    sp.wait_ge(y_taken, EX * (t - 1) + half + 1)
                sp.dma_start(gate_bc[:, 0:half, :], m["gate_dram"][0:half, :].partition_broadcast(P)).then_inc(gates_a, 16)
                if not first(t):
                    sp.wait_ge(y_taken, EX * t)
                sp.dma_start(gate_bc[:, half:, :], m["gate_dram"][half:, :].partition_broadcast(P)).then_inc(gates_b, 16)

            def store_x(t):
                sp.wait_ge(x_updated, t + 1)
                sp.dma_start(m["out_dram"][:, ds(SUB * t, SUB), :], x[:, ds(SUB * t, SUB), :]).then_inc(stored, 16)

            if load:
                sp.dma_start(x[:, 0:SUB, :], m["x_dram"][:, 0:SUB, :]).then_inc(loaded_x0, 16)
                for dst, src in ((const[:], m["const_dram"]), (wr[:], m["wr_dram"]),
                                 (b_up[:], m["b_up_dram"]), (b_down[:], m["b_down_dram"])):
                    sp.dma_start(dst, src).then_inc(loaded_small, 16)
                for e in range(EX):
                    if e >= 2:
                        sp.wait_ge(w_lo_done, e - 1)
                    up, down = m["w_dram"][e]
                    sp.dma_start(stage[e % 2][:, 0:HID], up).then_inc(loaded_w[e], 16)
                    sp.dma_start(stage[e % 2][:, HID:].rearrange("p (c n) -> p c n", c=CH), down)\
                      .then_inc(loaded_w[e], 16)
                    if e == 0:
                        sp.dma_start(x[:, SUB:2 * SUB, :], m["x_dram"][:, SUB:2 * SUB, :]).then_inc(loaded_x1, 16)
                    if e == 2:
                        spread_gates(0)
                sp.dma_start(x[:, 2 * SUB:, :], m["x_dram"][:, 2 * SUB:, :]).then_inc(loaded_x, 16)
            else:
                spread_gates(0)

            def tile(t):
                spread_gates(t + 1)
                if store:
                    store_x(t)

            tile(0)
            with sp.Fori(1, tiles - 1) as t:
                tile(t)
            if store:
                store_x(tiles - 1)
                sp.wait_ge(stored, 16 * tiles)
            sp.wait_ge(gates_out, 16 * tiles)

        @block.tensor
        def _(pe):
            def prep_turn(t):
                pe.wait_ge(xn_done, SUB * (t + 1))
                if not isinstance(t, int) or t > 1:
                    pe.wait_ge(x_updated, t - 1)
                for j in range(SUB):
                    last = pe.transpose(t_ps[:, j * P:(j + 1) * P], xn[:, j, :], ident)
                last.then_inc(xn_turned, 1)

            def prep_logits(t):
                pe.wait_ge(xf_done, t + 1)
                if not first(t):
                    pe.wait_ge(gate_t_done, t)
                for j in range(SUB):
                    last = pe.matmul(r_ps[:, j * NE:(j + 1) * NE], xf[:, j * P:(j + 1) * P], wr[:],
                                     start=True, stop=True)
                last.then_inc(logits_done, 1)

            def prep_gates(t):
                pe.wait_ge(router_step, ROUTER * (t + 1))
                for j in range(SUB):
                    last = pe.transpose(r_ps[0:EX, j * P:(j + 1) * P], gate[:, j, :], ident)
                last.then_inc(gate_turned, 1)

            def up(t, e):
                if e == 0:
                    pe.wait_ge(xs_done, t + 1)
                if load and first(t):
                    pe.wait_ge(w_lo_done, e + 1)
                for c in range(CH):
                    q = CH * e + c
                    if not first(t) or q >= UP_RING:
                        pe.wait_ge(gelu_done, EX * CH * t + q - UP_RING + 1)
                    bank = up_ps[q % UP_RING]
                    hi, lo = w_hi[:, e, c * P:(c + 1) * P], w_lo[:, e, c * P:(c + 1) * P]
                    pe.matmul(bank[:], hi, x_hi[:], start=True, stop=False)
                    pe.matmul(bank[:], hi, x_lo[:], start=False, stop=False)
                    pe.matmul(bank[:], lo, x_hi[:], start=False, stop=True).then_inc(up_done, 1)

            def down(t, e):
                bank = y_ps[e % Y_RING]
                if not first(t) or e >= Y_RING:
                    pe.wait_ge(y_taken, EX * t + e - Y_RING + 1)
                if e == 0:
                    pe.wait_ge(gate_t_done, t + 1)
                    pe.matmul(bank[:], b_down[:], gate_t[:], start=True, stop=False)
                for c in range(CH):
                    half = 2 * e + c // 2
                    if c % 2 == 0:
                        pe.wait_ge(lo_done, 2 * EX * t + half + 1)
                    cols = slice((c % 2) * TOK, (c % 2 + 1) * TOK)
                    hi = w_hi[:, e, HID + c * P:HID + (c + 1) * P]
                    lo = w_lo[:, e, HID + c * P:HID + (c + 1) * P]
                    a_hi, a_lo = h_hi[half % HL_RING][:, cols], h_lo[half % HL_RING][:, cols]
                    pe.matmul(bank[:], hi, a_hi, start=(c == 0 and e > 0), stop=False)
                    pe.matmul(bank[:], hi, a_lo, start=False, stop=False)
                    last = pe.matmul(bank[:], lo, a_hi, start=False, stop=(c == CH - 1))
                last.then_inc(down_done, 1)

            def turn_back(t):
                pe.wait_ge(acc_added, NE * (t + 1))
                if is_last(t):
                    pe.wait_ge(x_updated, t)
                else:
                    pe.wait_ge(xf_done, t + 2)
                for j in range(SUB):
                    last = pe.transpose(t_ps[:, j * P:(j + 1) * P], acc[:, j * P:(j + 1) * P], ident)
                last.then_inc(acc_turned, 1)

            def is_last(t):
                return isinstance(t, int) and t == tiles - 1

            def tile(t, prep=True):
                for e in range(EX):
                    up(t, e)
                    if e:
                        down(t, e - 1)
                    elif not first(t):
                        down(t - 1, EX - 1)
                    if e == 1 and not first(t):
                        turn_back(t - 1)
                    if prep:
                        if e == 3:
                            prep_turn(t + 1)
                        if e == 4:
                            prep_logits(t + 1)
                        if e == 6:
                            prep_gates(t + 1)

            pe.wait_ge(preset, 1)
            if load:
                pe.wait_ge(loaded_small, 64)
            prep_turn(0)
            prep_logits(0)
            prep_gates(0)
            tile(0)
            with pe.Fori(1, tiles - 1) as t:
                tile(t)
            tile(tiles - 1, prep=False)
            down(tiles - 1, EX - 1)
            turn_back(tiles - 1)

        @block.scalar
        def _(act):
            def prep_take(t):
                act.wait_ge(xn_turned, t + 1)
                if not first(t):
                    act.wait_ge(xs_done, t)
                    act.wait_ge(logits_done, t)
                act.activation(xf[:], t_ps[:], ACT.Copy).then_inc(xf_done, 1)

            def prep_gates(t):
                act.wait_ge(gate_turned, t + 1)
                if not first(t):
                    act.wait_ge(gates_out, 16 * t)
                    act.wait_ge(down_done, EX * (t - 1) + 1)
                act.activation(gate_t[:], r_ps[0:EX, :], ACT.Copy).then_inc(gate_t_done, 1)

            def split_weights(e):
                act.wait_ge(loaded_w[e], 32)
                act.activation(w_hi[:, e, :], stage[e % 2][:], ACT.Copy).then_inc(w_hi_done, 1)

            def tile(t, prep=True):
                for e in range(EX):
                    if prep:
                        if e == 4:
                            prep_take(t + 1)
                        if e == 7:
                            prep_gates(t + 1)
                    for s in range(2):
                        half = 2 * e + s
                        buf = h[half % H_RING]
                        if not first(t) or half >= H_RING:
                            act.wait_ge(lo_done, 2 * EX * t + half - H_RING + 1)
                        for k in range(2):
                            q = 2 * half + k
                            act.wait_ge(up_done, EX * CH * t + q + 1)
                            act.activation(buf[:, k * TOK:(k + 1) * TOK], up_ps[q % UP_RING][:],
                                           ACT.Gelu_apprx_tanh, bias=b_up[:, CH * e + q % CH:CH * e + q % CH + 1])\
                               .then_inc(gelu_done, 1)
                        act.wait_ge(gelu_done, EX * CH * t + 2 * half + 2)
                        if not first(t) or half >= HL_RING:
                            act.wait_ge(down_done, EX * t + e - HL_RING // 2 + 1)
                        act.activation(h_hi[half % HL_RING][:], buf[:], ACT.Copy).then_inc(hi_done, 1)
                    if load and first(t) and e + 1 < EX:
                        split_weights(e + 1)

            if load:
                split_weights(0)
            prep_take(0)
            prep_gates(0)
            tile(0)
            with act.Fori(1, tiles - 1) as t:
                tile(t)
            tile(tiles - 1, prep=False)

        @block.vector
        def _(dve):
            def prep_stats(t):
                if load:
                    if isinstance(t, int) and t < 2:
                        dve.wait_ge((loaded_x0, loaded_x1)[t], 16)
                    else:
                        dve.wait_ge(loaded_x, 16)
                if not first(t):
                    dve.wait_ge(rstd_done, t)
                    dve.wait_ge(xn_done, SUB * t)
                for j in range(SUB):
                    dve.bn_stats(stats[:, j, :], x[:, ds(SUB * t + j, 1), :].squeeze(1)).then_inc(stats_step, 1)
                dve.wait_ge(stats_step, STATS * t + SUB)
                dve.memset(carrier[:], 0.0)
                for j in range(SUB):
                    dve.bn_aggr(mv[:, j, :], stats[:, j, :]).then_inc(stats_step, 1)

            def prep_normalise(t):
                dve.wait_ge(rstd_done, t + 1)
                dve.wait_ge(stats_step, STATS * (t + 1))
                if not first(t):
                    dve.wait_ge(xn_turned, t)
                for j in range(SUB):
                    dve.tensor_scalar(xn[:, j, :], x[:, ds(SUB * t + j, 1), :].squeeze(1), mv[:, j, 0:1],
                                      rstd[:, j:j + 1], ALU.subtract, ALU.mult).then_inc(xn_done, 1)

            def prep_split(t):
                dve.wait_ge(xf_done, t + 1)
                if not first(t):
                    dve.wait_ge(up_done, EX * CH * t)
                dve.tensor_copy(x_hi[:], xf[:]).then_inc(xs_hi, 1)
                dve.wait_ge(xs_hi, t + 1)
                dve.tensor_tensor(x_lo[:], xf[:], x_hi[:].bitcast(F32), ALU.subtract).then_inc(xs_done, 1)

            def router_top(t):
                base = ROUTER * t
                dve.wait_ge(logits_done, t + 1)
                if not first(t):
                    dve.wait_ge(router_step, base)
                dve.tensor_copy(logits[:].rearrange("p j e -> p (j e)"), r_ps[:, 0:SUB * NE]).then_inc(router_step, 1)
                dve.wait_ge(router_step, base + 1)
                dve.memset(carrier[:], 0.0)
                for j in range(SUB):
                    dve.max(top[:, j, :], logits[:, j, :]).then_inc(router_step, 1)
                dve.wait_ge(router_step, base + 1 + SUB)
                dve.memset(carrier[:], 0.0)
                for j in range(SUB):
                    dve.max_index(topi[:, j, :], top[:, j, :], logits[:, j, :]).then_inc(router_step, 1)
                dve.tensor_tensor(gap[:], top[:, :, 1], top[:, :, 0], ALU.subtract).then_inc(router_step, 1)

            def router_gates(t):
                base = ROUTER * t + 2 + 2 * SUB
                wide = [P, SUB, NE]
                iota = const[:, C_IOTA:C_IOTA + NE].unsqueeze(1).to_broadcast(wide)
                dve.wait_ge(egap_done, t + 1)
                if not first(t):
                    dve.wait_ge(gate_turned, t)
                dve.wait_ge(router_step, base)
                dve.tensor_tensor(eq1[:], topi[:, :, 0:1].to_broadcast(wide), iota, ALU.is_equal)
                dve.tensor_tensor(eq2[:], topi[:, :, 1:2].to_broadcast(wide), iota, ALU.is_equal)
                dve.tensor_scalar(egap1[:], egap[:], 1.0, None, ALU.add).then_inc(router_step, 1)
                dve.wait_ge(router_step, base + 1)
                dve.reciprocal(g1[:], egap1[:]).then_inc(router_step, 1)
                dve.wait_ge(router_step, base + 2)
                dve.tensor_tensor(g2[:], egap[:], g1[:], ALU.mult)
                dve.tensor_tensor(eq1[:], eq1[:], g1[:].unsqueeze(2).to_broadcast(wide), ALU.mult).then_inc(router_step, 1)
                dve.wait_ge(router_step, base + 3)
                dve.tensor_tensor(eq2[:], eq2[:], g2[:].unsqueeze(2).to_broadcast(wide), ALU.mult).then_inc(router_step, 1)
                dve.wait_ge(router_step, base + 4)
                dve.tensor_tensor(gate[:, :, 0:NE], eq1[:], eq2[:], ALU.add).then_inc(router_step, 1)

            def lo(t, half):
                dve.wait_ge(hi_done, 2 * EX * t + half + 1)
                if not first(t) or half >= HL_RING:
                    dve.wait_ge(down_done, EX * t + half // 2 - HL_RING // 2 + 1)
                dve.tensor_tensor(h_lo[half % HL_RING][:], h[half % H_RING][:],
                                  h_hi[half % HL_RING][:].bitcast(F32), ALU.subtract).then_inc(lo_done, 1)

            def take(t, e):
                dve.wait_ge(down_done, EX * t + e + 1)
                if e == 0:
                    if not first(t):
                        dve.wait_ge(acc_turned, t)
                    dve.tensor_copy(acc[:], y_ps[0][:]).then_inc(y_taken, 1)
                    return
                if e == 1:
                    dve.wait_ge(gates_a, 16 * (t + 1))
                if e == NE // 2 + 1:
                    dve.wait_ge(gates_b, 16 * (t + 1))
                if not first(t) or e > T_RING:
                    dve.wait_ge(acc_added, NE * t + e - T_RING)
                dve.tensor_tensor(gated[e % T_RING][:], y_ps[e % Y_RING][:], gate_bc[:, e - 1, :], ALU.mult)\
                   .then_inc(y_taken, 1)

            def update(t):
                dve.wait_ge(acc_turned, t + 1)
                rows = x[:, ds(SUB * t, SUB), :].rearrange("p j c -> p (j c)")
                dve.scalar_tensor_tensor(rows, t_ps[:], 0.5, rows, ALU.mult, ALU.add).then_inc(x_updated, 1)

            def split_weights(e):
                dve.wait_ge(w_hi_done, e + 1)
                dve.tensor_tensor(w_lo[:, e, :], stage[e % 2][:], w_hi[:, e, :].bitcast(F32), ALU.subtract)\
                   .then_inc(w_lo_done, 1)

            def tile(t, prep=True):
                for e in range(EX):
                    lo(t, 2 * e)
                    if prep and e == EX - 1:
                        prep_split(t + 1)
                    lo(t, 2 * e + 1)
                    if load and first(t) and e + 1 < EX:
                        split_weights(e + 1)
                    if e:
                        take(t, e - 1)
                    elif not first(t):
                        take(t - 1, EX - 1)
                    if e == 2 and not first(t):
                        update(t - 1)
                    if prep:
                        if e == 1:
                            prep_stats(t + 1)
                        if e == 2:
                            prep_normalise(t + 1)
                        if e == 4:
                            router_top(t + 1)
                        if e == 5:
                            router_gates(t + 1)

            dve.memset(half_neg[:], -0.5)
            dve.memset(eps[:], LN_EPS)
            dve.memset(euler[:], float(np.e))
            dve.memset(gate[:, :, NE:EX], 1.0).then_inc(preset, 1)
            if load:
                dve.wait_ge(loaded_small, 64)
            prep_stats(0)
            prep_normalise(0)
            if load:
                split_weights(0)
            router_top(0)
            prep_split(0)
            router_gates(0)
            tile(0)
            with dve.Fori(1, tiles - 1) as t:
                tile(t)
            tile(tiles - 1, prep=False)
            take(tiles - 1, EX - 1)
            update(tiles - 1)

        @block.gpsimd
        def _(pool):
            def prep_rstd(t):
                pool.wait_ge(stats_step, STATS * (t + 1))
                if not first(t):
                    pool.wait_ge(xn_done, SUB * t)
                pool.tensor_tensor(veps[:], mv[:, :, 1], eps[:], ALU.add).then_inc(var_eps, 1)
                pool.wait_ge(var_eps, t + 1)
                pool.tensor_tensor(rstd[:], veps[:], half_neg[:], ALU.pow).then_inc(rstd_done, 1)

            def router_exp(t):
                pool.wait_ge(router_step, ROUTER * t + 2 + 2 * SUB)
                pool.tensor_tensor(egap[:], euler[:], gap[:], ALU.pow).then_inc(egap_done, 1)

            def add(t, e):
                pool.wait_ge(y_taken, EX * t + e + 1)
                if not first(t) or e > 1:
                    pool.wait_ge(acc_added, NE * t + e - 1)
                pool.tensor_tensor(acc[:], acc[:], gated[e % T_RING][:], ALU.add).then_inc(acc_added, 1)

            def tile(t, prep=True):
                for e in range(EX):
                    if e >= 2:
                        add(t, e - 1)
                    elif e == 0 and not first(t):
                        add(t - 1, EX - 1)
                    if prep:
                        if e == 1:
                            prep_rstd(t + 1)
                        if e == 4:
                            router_exp(t + 1)

            pool.wait_ge(preset, 1)
            prep_rstd(0)
            router_exp(0)
            tile(0)
            with pool.Fori(1, tiles - 1) as t:
                tile(t)
            tile(tiles - 1, prep=False)
            add(tiles - 1, EX - 1)

PAIRS = HEADS // 2
QT = 4
S_RING, M_RING, A_RING, F_RING = 2, 2, 2, 2


def retention_phase(nc, m):
    seqs = m["tokens"] // SEQ
    TB = SEQ // P
    ctx = ExitStack()
    with ctx:
        def sb(n, shape, dt=F32):
            return ctx.enter_context(nc.sbuf_tensor(f"ret_{n}", shape, dt))

        def pb(n, shape):
            return ctx.enter_context(nc.psum_tensor(f"ret_{n}", shape, F32))

        def sem(n):
            return ctx.enter_context(nc.semaphore(f"ret_{n}"))

        x, const = m["x"], m["const"]
        ident = const[:, C_ID:C_ID + P]
        mask = sb("mask", [P, HEADS, CAUSAL])
        wqk_hi = sb("wqk_hi", [P, 2 * QT * P], F32R)
        wqk_lo = sb("wqk_lo", [P, 2 * QT * P], F32R)
        wvg_hi = sb("wvg_hi", [P, 2 * VB], F32R)
        wvg_lo = sb("wvg_lo", [P, 2 * VB], F32R)
        wo = sb("wo", [P, VB // P, P])
        bqk = sb("bqk", [P, 2 * QT])
        bvg = sb("bvg", [P, 2 * VB])
        bo = sb("bo", [P, P])
        f = sb("f", [P, F_RING, 2, SEQ])
        qk = [sb(f"qk{i}", [P, 2 * QT, SEQ], F32R) for i in range(2)]
        vg = [sb(f"vg{i}", [P, TB, 2 * VB]) for i in range(2)]
        masked = [sb(f"masked{i}", [P, 2, CAUSAL]) for i in range(M_RING)]
        absed = [sb(f"absed{i}", [P, 2, CAUSAL]) for i in range(A_RING)]
        abs_hi = [sb(f"abs_hi{i}", [P, 2, CAUSAL], F32R) for i in range(A_RING)]
        abs_lo = [sb(f"abs_lo{i}", [P, 2, CAUSAL], F32R) for i in range(A_RING)]
        pick = sb("pick", [P, P + HEADS - 1], F32R)
        sums = sb("sums", [HEADS, CAUSAL])
        xn = sb("xn", [P, TB, P])
        x_hi = sb("x_hi", [P, SEQ], F32R)
        x_lo = sb("x_lo", [P, SEQ], F32R)
        stats = sb("stats", [P, TB, 6])
        mv = sb("mv", [P, TB, 2])
        veps = sb("veps", [P, TB])
        rstd = sb("rstd", [P, TB])
        eps = sb("eps", [P, TB])
        carrier = sb("carrier", [P, 1])
        half_neg = sb("half_neg", [P, TB * HEADS])
        ones = sb("ones", [P, 1])
        r_sb = sb("r_sb", [P, TB * VB])
        square = sb("square", [P, TB * VB])
        denom = sb("denom", [P, TB * HEADS])
        denom2 = sb("denom2", [P, TB * HEADS])
        ssum = sb("ssum", [P, TB * HEADS])
        power = sb("power", [P, TB * HEADS])
        rms = sb("rms", [P, TB * HEADS])
        gated_t = square

        s_ps = pb("s", [P, S_RING, 2, 512])
        r_ps = pb("r", [P, TB * VB])
        a_ps = pb("a", [P, 512])
        t_ps = pb("t", [P, 512])
        p_ps = pb("p", [P, 2, SEQ])

        loaded, loaded_mask = sem("loaded"), sem("loaded_mask")
        split_hi, split_lo, preset = sem("split_hi"), sem("split_lo"), sem("preset")
        stats_step, var_eps, rstd_done, xn_done = sem("stats_step"), sem("var_eps"), sem("rstd_done"), sem("xn_done")
        bias_added = sem("bias_added")
        xn_turned, x_hi_done, x_lo_done = sem("xn_turned"), sem("x_hi_done"), sem("x_lo_done")
        projected, f_done, qk_hi, qk_done, vg_done = sem("projected"), sem("f_done"), sem("qk_hi"), sem("qk_done"), sem("vg_done")
        scored, mask_done, mixed = sem("scored"), sem("mask_done"), sem("mixed")
        abs_done, abs_hi_done, abs_lo_done, summed = sem("abs_done"), sem("abs_hi_done"), sem("abs_lo_done"), sem("summed")
        sums_taken, sums_turned = sem("sums_taken"), sem("sums_turned")
        r_taken, square_done = sem("r_taken"), sem("square_done")
        norm_step, rms_done = sem("norm_step"), sem("rms_done")
        gated_turned, gated_t_done, out_done, x_updated = sem("gated_turned"), sem("gated_t_done"), sem("out_done"), sem("x_updated")
        STATS, NORM = 2 * TB, 6
        VG_ITEMS = TB
        ITEMS = QT + VG_ITEMS
        block = ctx.enter_context(nc.Block())

        def first(b):
            return isinstance(b, int) and b == 0

        @block.sync
        def _(sp):
            for dst, src in ((f[:].rearrange("p r k s -> p (r k s)"), m["w_qk_dram"]),
                             (vg[0][:, 0, :], m["w_vg_dram"]), (wo[:], m["w_o_dram"]), (bqk[:], m["b_qk_dram"]),
                             (bvg[:], m["b_vg_dram"].partition_broadcast(P)),
                             (bo[:], m["b_o_dram"].partition_broadcast(P))):
                sp.dma_start(dst, src).then_inc(loaded, 16)
            sp.dma_start(mask[:], m["mask_dram"]).then_inc(loaded_mask, 16)

        @block.tensor
        def _(pe):
            def turn(b):
                pe.wait_ge(xn_done, TB * (b + 1))
                if not isinstance(b, int) or b > 2:
                    pe.wait_ge(x_updated, b - 2)
                for j in range(TB):
                    last = pe.transpose(t_ps[:, j * P:(j + 1) * P], xn[:, j, :], ident)
                last.then_inc(xn_turned, 1)

            def project_qk(b, g):
                if g == 0:
                    pe.wait_ge(x_lo_done, b + 1)
                if not first(b) or g:
                    wait_bank(b, g)
                for k in range(2):
                    cols = slice((2 * g + k) * P, (2 * g + k + 1) * P)
                    pe.matmul(p_ps[:, k, :], wqk_hi[:, cols], x_hi[:], start=True, stop=False)
                    pe.matmul(p_ps[:, k, :], wqk_hi[:, cols], x_lo[:], start=False, stop=False)
                    last = pe.matmul(p_ps[:, k, :], wqk_lo[:, cols], x_hi[:], start=False, stop=True)
                last.then_inc(projected, 1)

            def project_vg(b, j):
                wait_bank(b, QT + j)
                out = p_ps[:].rearrange("p a b -> p (a b)")
                hi, lo = x_hi[:, j * P:(j + 1) * P], x_lo[:, j * P:(j + 1) * P]
                pe.matmul(out, hi, wvg_hi[:], start=True, stop=False)
                pe.matmul(out, hi, wvg_lo[:], start=False, stop=False)
                pe.matmul(out, lo, wvg_hi[:], start=False, stop=True).then_inc(projected, 1)

            def wait_bank(b, item):
                if item == 0:
                    pe.wait_ge(vg_done, VG_ITEMS * b)
                elif item <= QT:
                    pe.wait_ge(f_done, 2 * (QT * b + item))
                else:
                    pe.wait_ge(vg_done, VG_ITEMS * b + item - QT)

            def scores(b, par, p):
                pe.wait_ge(qk_done, QT * b + p // 2 + 1)
                if not first(b) or p >= S_RING:
                    pe.wait_ge(mask_done, PAIRS * b + p - S_RING + 1)
                for i in range(2):
                    g, j = (2 * p + i) // 4, (2 * p + i) % 4
                    rows = slice(32 * j, 32 * j + 32)
                    q, k = qk[par][rows, 2 * g, :], qk[par][rows, 2 * g + 1, :]
                    pe.matmul(s_ps[:, p % S_RING, i, 0:SEQ], k[:, P:SEQ], q, start=True, stop=True)
                    last = pe.matmul(s_ps[:, p % S_RING, i, SEQ:2 * SEQ], k[:, 0:P], q, start=True, stop=True)
                last.then_inc(scored, 1)

            def mix(b, par, p):
                pe.wait_ge(mask_done, PAIRS * b + p + 1)
                if p == 0:
                    pe.wait_ge(vg_done, VG_ITEMS * (b + 1))
                    if not first(b):
                        pe.wait_ge(square_done, b)
                for i in range(2):
                    h = 2 * p + i
                    v0, v1 = (vg[par][:, j, h * VD:(h + 1) * VD] for j in range(TB))
                    o0, o1 = (r_ps[:, j * VB + h * VD:j * VB + (h + 1) * VD] for j in range(TB))
                    src = masked[p % M_RING]
                    pe.matmul(o0, src[:, i, P:2 * P], v0, start=True, stop=True)
                    pe.matmul(o1, src[:, i, 2 * P:3 * P], v0, start=True, stop=False)
                    last = pe.matmul(o1, src[:, i, 0:P], v1, start=False, stop=True)
                last.then_inc(mixed, 1)

            def add_up(b, p):
                pe.wait_ge(abs_lo_done, PAIRS * b + p + 1)
                if p == 0 and not first(b):
                    pe.wait_ge(sums_taken, b)
                for i in range(2):
                    h = 2 * p + i
                    one = pick[:, HEADS - 1 - h:HEADS - 1 - h + P]
                    out = a_ps[:, 0:CAUSAL]
                    pe.matmul(out, one, abs_hi[p % A_RING][:, i, :], start=(h == 0), stop=False)
                    last = pe.matmul(out, one, abs_lo[p % A_RING][:, i, :], start=False, stop=(h == HEADS - 1))
                last.then_inc(summed, 1)

            def turn_sums(b):
                pe.wait_ge(sums_taken, b + 1)
                if isinstance(b, int) and b >= seqs - 2:
                    pe.wait_ge(x_updated, b)
                else:
                    pe.wait_ge(x_lo_done, b + 3)
                one = ident[0:HEADS, 0:HEADS]
                pe.matmul(t_ps[:, 0:HEADS], sums[:, P:2 * P], one, start=True, stop=True)
                pe.matmul(t_ps[:, HEADS:2 * HEADS], sums[:, 2 * P:3 * P], one, start=True, stop=False)
                pe.matmul(t_ps[:, HEADS:2 * HEADS], sums[:, 0:P], one, start=False, stop=True).then_inc(sums_turned, 1)

            def turn_gated(b):
                pe.wait_ge(norm_step, NORM * (b + 1))
                for j in range(TB):
                    for k in range(VB // P):
                        last = pe.transpose(t_ps[:, k * SEQ + j * P:k * SEQ + (j + 1) * P],
                                            r_sb[:, j * VB + k * P:j * VB + (k + 1) * P], ident)
                last.then_inc(gated_turned, 1)

            def project_out(b):
                pe.wait_ge(gated_t_done, b + 1)
                for j in range(TB):
                    for k in range(VB // P):
                        last = pe.matmul(t_ps[:, j * P:(j + 1) * P], gated_t[:, k * SEQ + j * P:k * SEQ + (j + 1) * P],
                                         wo[:, k, :], start=(k == 0), stop=(k == VB // P - 1))
                last.then_inc(out_done, 1)

            def sequence(b, par, prep=True):
                for p in range(PAIRS):
                    scores(b, par, p)
                    if p:
                        mix(b, par, p - 1)
                    elif not first(b):
                        mix(b - 1, 1 - par, PAIRS - 1)
                    if p >= 2:
                        add_up(b, p - 2)
                    elif not first(b):
                        add_up(b - 1, PAIRS - 2 + p)
                    if prep:
                        if p == 0:
                            turn(b + 1)
                        elif p <= QT:
                            project_qk(b + 1, p - 1)
                        elif p <= ITEMS:
                            project_vg(b + 1, p - QT - 1)
                    if not first(b):
                        if p == 2:
                            turn_sums(b - 1)
                        if p == 5:
                            turn_gated(b - 1)
                        if p == 7:
                            project_out(b - 1)

            pe.wait_ge(preset, 3)
            pe.wait_ge(split_lo, 2)
            turn(0)
            for g in range(QT):
                project_qk(0, g)
            for j in range(TB):
                project_vg(0, j)
            sequence(0, 0)
            sequence(1, 1)
            with pe.Fori(1, seqs // 2 - 1) as two:
                sequence(2 * two, 0)
                sequence(2 * two + 1, 1)
            sequence(seqs - 2, 0)
            sequence(seqs - 1, 1, prep=False)
            mix(seqs - 1, 1, PAIRS - 1)
            add_up(seqs - 1, PAIRS - 2)
            add_up(seqs - 1, PAIRS - 1)
            turn_sums(seqs - 1)
            turn_gated(seqs - 1)
            project_out(seqs - 1)

        
        @block.scalar
        def _(act):
            def take_x(b):
                act.wait_ge(xn_turned, b + 1)
                if not first(b):
                    act.wait_ge(projected, ITEMS * b)
                act.activation(x_hi[:], t_ps[:, 0:SEQ], ACT.Copy).then_inc(x_hi_done, 1)

            def take_qk(b, g):
                act.wait_ge(projected, ITEMS * b + g + 1)
                if not first(b) or g >= F_RING:
                    act.wait_ge(qk_done, QT * b + g - F_RING + 1)
                for k in range(2):
                    act.activation(f[:, g % F_RING, k, :], p_ps[:, k, :], ACT.Identity,
                                   bias=bqk[:, 2 * g + k:2 * g + k + 1]).then_inc(f_done, 1)

            def magnitudes(b, p):
                act.wait_ge(mask_done, PAIRS * b + p + 1)
                if not first(b) or p >= A_RING:
                    act.wait_ge(abs_lo_done, PAIRS * b + p - A_RING + 1)
                act.activation(absed[p % A_RING][:], masked[p % M_RING][:], ACT.Abs).then_inc(abs_done, 1)
                act.wait_ge(abs_done, PAIRS * b + p + 1)
                if not first(b) or p >= A_RING:
                    act.wait_ge(summed, PAIRS * b + p - A_RING + 1)
                act.activation(abs_hi[p % A_RING][:], absed[p % A_RING][:], ACT.Copy).then_inc(abs_hi_done, 1)

            def take_r(b):
                act.wait_ge(mixed, PAIRS * (b + 1))
                if not first(b):
                    act.wait_ge(gated_turned, b)
                act.activation(r_sb[:], r_ps[:], ACT.Copy).then_inc(r_taken, 1)
                if not first(b):
                    act.wait_ge(out_done, b)
                act.activation(square[:], r_ps[:], ACT.Square).then_inc(square_done, 1)

            def take_sums(b):
                act.wait_ge(summed, PAIRS * (b + 1))
                if not first(b):
                    act.wait_ge(sums_turned, b)
                act.activation(sums[:], a_ps[0:HEADS, 0:CAUSAL], ACT.Copy).then_inc(sums_taken, 1)

            def take_gated(b):
                act.wait_ge(gated_turned, b + 1)
                act.activation(gated_t[:], t_ps[:], ACT.Copy).then_inc(gated_t_done, 1)

            def sequence(b, prep=True):
                for p in range(PAIRS):
                    if p == 2 and not first(b):
                        take_sums(b - 1)
                    magnitudes(b, p)
                    if p == 0 and not first(b):
                        take_r(b - 1)
                    if prep:
                        if p == 0:
                            take_x(b + 1)
                        elif p <= QT:
                            take_qk(b + 1, p - 1)
                    if p == 5 and not first(b):
                        take_gated(b - 1)

            act.wait_ge(loaded, 96)
            act.activation(wqk_hi[:], f[:].rearrange("p r k s -> p (r k s)"), ACT.Copy).then_inc(split_hi, 1)
            act.activation(wvg_hi[:], vg[0][:, 0, :], ACT.Copy).then_inc(split_hi, 1)
            take_x(0)
            act.wait_ge(split_lo, 2)
            for g in range(QT):
                take_qk(0, g)
            sequence(0)
            sequence(1)
            with act.Fori(1, seqs // 2 - 1) as two:
                sequence(2 * two)
                sequence(2 * two + 1)
            sequence(seqs - 2)
            sequence(seqs - 1, prep=False)
            take_r(seqs - 1)
            take_sums(seqs - 1)
            take_gated(seqs - 1)

        @block.vector
        def _(dve):
            def prep_stats(b):
                if not first(b):
                    dve.wait_ge(rstd_done, b)
                    dve.wait_ge(xn_done, TB * b)
                for j in range(TB):
                    dve.bn_stats(stats[:, j, :], x[:, ds(TB * b + j, 1), :].squeeze(1)).then_inc(stats_step, 1)
                dve.wait_ge(stats_step, STATS * b + TB)
                dve.memset(carrier[:], 0.0)
                for j in range(TB):
                    dve.bn_aggr(mv[:, j, :], stats[:, j, :]).then_inc(stats_step, 1)

            def prep_normalise(b):
                dve.wait_ge(rstd_done, b + 1)
                dve.wait_ge(stats_step, STATS * (b + 1))
                if not first(b):
                    dve.wait_ge(xn_turned, b)
                for j in range(TB):
                    dve.tensor_scalar(xn[:, j, :], x[:, ds(TB * b + j, 1), :].squeeze(1), mv[:, j, 0:1],
                                      rstd[:, j:j + 1], ALU.subtract, ALU.mult).then_inc(xn_done, 1)

            def split_x(b):
                dve.wait_ge(x_hi_done, b + 1)
                dve.tensor_tensor(x_lo[:], t_ps[:, 0:SEQ], x_hi[:].bitcast(F32), ALU.subtract).then_inc(x_lo_done, 1)

            def split_qk(b, par, g):
                dve.wait_ge(qk_hi, QT * b + g + 1)
                for k in range(2):
                    part = qk[par][:, 2 * g + k, :]
                    low = const[:, C_QLOW + k:C_QLOW + k + 1]
                    last = dve.scalar_tensor_tensor(part, part.bitcast(F32), low, f[:, g % F_RING, k, :], ALU.mult, ALU.add)
                last.then_inc(qk_done, 1)

            def take_vg(b, par, j):
                dve.wait_ge(projected, ITEMS * b + QT + j + 1)
                if not first(b) and not (isinstance(b, int) and b < 2):
                    dve.wait_ge(mixed, PAIRS * (b - 1))
                    dve.wait_ge(norm_step, NORM * (b - 1))
                dve.tensor_tensor(vg[par][:, j, :], p_ps[:].rearrange("p a b -> p (a b)"), bvg[:], ALU.add)\
                   .then_inc(vg_done, 1)

            def apply_mask(b, p):
                dve.wait_ge(scored, PAIRS * b + p + 1)
                if not first(b) or p >= M_RING:
                    dve.wait_ge(mixed, PAIRS * b + p - M_RING + 1)
                    dve.wait_ge(abs_done, PAIRS * b + p - M_RING + 1)
                dve.tensor_tensor(masked[p % M_RING][:], s_ps[:, p % S_RING, :, P:4 * P], mask[:, 2 * p:2 * p + 2, :],
                                  ALU.mult).then_inc(mask_done, 1)

            def abs_low(b, p):
                dve.wait_ge(abs_hi_done, PAIRS * b + p + 1)
                if not first(b) or p >= A_RING:
                    dve.wait_ge(summed, PAIRS * b + p - A_RING + 1)
                dve.tensor_tensor(abs_lo[p % A_RING][:], absed[p % A_RING][:], abs_hi[p % A_RING][:].bitcast(F32),
                                  ALU.subtract).then_inc(abs_lo_done, 1)

            def norm_denominator(b):
                base = NORM * b
                dve.wait_ge(sums_turned, b + 1)
                if not first(b):
                    dve.wait_ge(norm_step, base)
                dve.tensor_scalar(denom[:], t_ps[:, 0:TB * HEADS], DENOM_LO, DENOM_HI, ALU.max, ALU.min).then_inc(norm_step, 1)
                dve.wait_ge(norm_step, base + 1)
                dve.scalar_tensor_tensor(denom2[:], denom[:], RMS_EPS, denom[:], ALU.mult, ALU.mult).then_inc(norm_step, 1)
                dve.wait_ge(square_done, b + 1)
                dve.tensor_reduce(ssum[:], square[:].rearrange("p (h d) -> p h d", d=VD), AX.X, ALU.add).then_inc(norm_step, 1)
                dve.wait_ge(norm_step, base + 3)
                dve.scalar_tensor_tensor(power[:], ssum[:], 1.0 / VD, denom2[:], ALU.mult, ALU.add).then_inc(norm_step, 1)

            def norm_apply(b, par):
                base = NORM * b + 4
                wide = r_sb[:].rearrange("p (h d) -> p h d", d=VD)
                dve.wait_ge(r_taken, b + 1)
                flat = r_sb[:].rearrange("p (j c) -> p j c", j=TB)
                dve.tensor_tensor(flat, flat, vg[par][:, :, VB:2 * VB], ALU.mult).then_inc(norm_step, 1)
                dve.wait_ge(rms_done, b + 1)
                dve.wait_ge(norm_step, base + 1)
                dve.tensor_tensor(wide, wide, rms[:].unsqueeze(2).to_broadcast([P, TB * HEADS, VD]), ALU.mult)\
                   .then_inc(norm_step, 1)

            def update(b):
                dve.wait_ge(out_done, b + 1)
                dve.wait_ge(bias_added, b + 1)
                rows = x[:, ds(TB * b, TB), :].rearrange("p j c -> p (j c)")
                dve.tensor_tensor(rows, t_ps[:, 0:SEQ], rows, ALU.add).then_inc(x_updated, 1)

            def sequence(b, par, prep=True):
                for p in range(PAIRS):
                    apply_mask(b, p)
                    if p:
                        abs_low(b, p - 1)
                    elif not first(b):
                        abs_low(b - 1, PAIRS - 1)
                    if prep:
                        if p == 0:
                            split_x(b + 1)
                        elif 2 <= p <= QT + 1:
                            split_qk(b + 1, 1 - par, p - 2)
                        if p == 5 or p == 6:
                            take_vg(b + 1, 1 - par, p - 5)
                        if p == 6 and not is_second_last(b):
                            prep_stats(b + 2)
                        if p == 7 and not is_second_last(b):
                            prep_normalise(b + 2)
                    if not first(b):
                        if p == 3:
                            norm_denominator(b - 1)
                        if p == 4:
                            norm_apply(b - 1, 1 - par)
                        if p == 7:
                            update(b - 1)

            def is_second_last(b):
                return isinstance(b, int) and b == seqs - 2

            dve.memset(half_neg[:], -0.5)
            dve.memset(eps[:], LN_EPS).then_inc(preset, 1)
            dve.memset(pick[:].bitcast(F32), 0.0).then_inc(preset, 1)
            dve.wait_ge(preset, 2)
            dve.memset(pick[:, HEADS - 1:HEADS].bitcast(F32), 1.0)
            dve.memset(ones[:], 1.0).then_inc(preset, 1)
            prep_stats(0)
            prep_normalise(0)
            for k, (lo, src, hi) in enumerate(((wqk_lo, f[:].rearrange("p r k s -> p (r k s)"), wqk_hi),
                                               (wvg_lo, vg[0][:, 0, :], wvg_hi))):
                dve.wait_ge(split_hi, k + 1)
                dve.tensor_tensor(lo[:], src, hi[:].bitcast(F32), ALU.subtract).then_inc(split_lo, 1)
            dve.wait_ge(split_lo, 2)
            split_x(0)
            for g in range(QT):
                split_qk(0, 0, g)
            for j in range(TB):
                take_vg(0, 0, j)
            prep_stats(1)
            prep_normalise(1)
            dve.wait_ge(loaded_mask, 16)
            sequence(0, 0)
            sequence(1, 1)
            with dve.Fori(1, seqs // 2 - 1) as two:
                sequence(2 * two, 0)
                sequence(2 * two + 1, 1)
            sequence(seqs - 2, 0)
            sequence(seqs - 1, 1, prep=False)
            abs_low(seqs - 1, PAIRS - 1)
            norm_denominator(seqs - 1)
            norm_apply(seqs - 1, 1)
            update(seqs - 1)

        @block.gpsimd
        def _(pool):
            def prep_rstd(b):
                pool.wait_ge(stats_step, STATS * (b + 1))
                if not first(b):
                    pool.wait_ge(xn_done, TB * b)
                pool.tensor_tensor(veps[:], mv[:, :, 1], eps[:], ALU.add).then_inc(var_eps, 1)
                pool.wait_ge(var_eps, b + 1)
                pool.tensor_tensor(rstd[:], veps[:], half_neg[:, 0:TB], ALU.pow).then_inc(rstd_done, 1)

            def add_bias(b):
                pool.wait_ge(xn_done, TB * (b + 1))
                rows = x[:, ds(TB * b, TB), :]
                pool.tensor_tensor(rows, rows, bo[:].unsqueeze(1).to_broadcast([P, TB, P]), ALU.add).then_inc(bias_added, 1)

            def qk_high(b, par, g):
                pool.wait_ge(f_done, 2 * (QT * b + g + 1))
                if not isinstance(b, int) or b > 1:
                    pool.wait_ge(scored, PAIRS * (b - 1))
                wide = [P, 2, SEQ]
                pool.tensor_tensor(qk[par][:, 2 * g:2 * g + 2, :], f[:, g % F_RING, :, :],
                                   ones[:].unsqueeze(2).to_broadcast(wide), ALU.mult).then_inc(qk_hi, 1)

            def rms_scale(b):
                pool.wait_ge(norm_step, NORM * b + 4)
                pool.tensor_tensor(rms[:], power[:], half_neg[:], ALU.pow).then_inc(rms_done, 1)

            def sequence(b, par, prep=True):
                for g in range(QT):
                    if g == 2 and not first(b):
                        rms_scale(b - 1)
                    if prep:
                        qk_high(b + 1, 1 - par, g)
                if prep:
                    if not (isinstance(b, int) and b == seqs - 2):
                        prep_rstd(b + 2)
                        add_bias(b + 2)

            pool.wait_ge(preset, 3)
            prep_rstd(0)
            pool.wait_ge(loaded, 96)
            add_bias(0)
            for g in range(QT):
                qk_high(0, 0, g)
            prep_rstd(1)
            add_bias(1)
            sequence(0, 0)
            sequence(1, 1)
            with pool.Fori(1, seqs // 2 - 1) as two:
                sequence(2 * two, 0)
                sequence(2 * two + 1, 1)
            sequence(seqs - 2, 0)
            sequence(seqs - 1, 1, prep=False)
            rms_scale(seqs - 1)


def build(nc, x, const, mask, w_qk, b_qk, w_vg, b_vg, w_o, b_o, wfc_s, wproj_s, wr, wfc, wproj, b_up, b_down,
          gate_scratch, out):
    tokens = x.shape[0]
    ctx = ExitStack()
    with ctx:
        def sb(n, shape, dt=F32):
            return ctx.enter_context(nc.sbuf_tensor(n, shape, dt))

        m = {
            "tokens": tokens,
            "x": sb("x", [P, tokens // P, P]),
            "w_hi": sb("w_hi", [P, EX, 2 * HID], F32R),
            "w_lo": sb("w_lo", [P, EX, 2 * HID], F32R),
            "const": sb("const", [P, C_END]),
            "wr": sb("wr", [P, NE]),
            "b_up": sb("b_up", [P, EX * CH]),
            "b_down": sb("b_down", [EX, P]),
            "x_dram": x.rearrange("(n p) c -> p n c", p=P),
            "out_dram": out.rearrange("(n p) c -> p n c", p=P),
            "const_dram": const, "wr_dram": wr, "b_up_dram": b_up, "b_down_dram": b_down,
            "w_dram": [(wfc_s, wproj_s.rearrange("(c p) n -> p c n", p=P))]
                      + [(wfc[e], wproj[e].rearrange("(c p) n -> p c n", p=P)) for e in range(NE)],
            "gate_dram": gate_scratch,
            "mask_dram": mask, "w_qk_dram": w_qk, "b_qk_dram": b_qk, "w_vg_dram": w_vg, "b_vg_dram": b_vg,
            "w_o_dram": w_o.rearrange("(k p) n -> p k n", p=P), "b_o_dram": b_o,
        }
        ffn_phase(nc, m, "ffn1", load=True, store=False)
        retention_phase(nc, m)
        ffn_phase(nc, m, "ffn2", load=False, store=True)


def decay_mask():
    gamma = np.log(1.0 - 2.0 ** (-5.0 - np.arange(HEADS)))
    at = np.arange(SEQ)
    diff = at[:, None] - at[None, :]
    decay = np.where(diff >= 0, np.exp(gamma[:, None, None] * np.maximum(diff, 0)), 0.0)
    full = (decay / np.sqrt(decay.sum(-1, keepdims=True))).transpose(2, 0, 1)
    blocks = (full[P:, :, P:], full[:P, :, :P], full[:P, :, P:])
    return np.ascontiguousarray(np.concatenate(blocks, axis=2)).astype(np.float32)


def constants():
    c = np.zeros((P, C_END), np.float32)
    c[:, C_ID:C_ID + P] = np.eye(P)
    c[:, C_IOTA:C_IOTA + NE] = np.arange(NE)
    copy = np.arange(P) // KD % 4
    c[:, C_QLOW] = np.where(copy >= 2, -1.0, 0.0)
    c[:, C_KLOW] = np.where(copy % 2 == 1, -1.0, 0.0)
    return c


def kernel(L0_attn_x, L0_attn_W_qk, L0_attn_b_qk, L0_attn_W_v, L0_attn_b_v, L0_attn_W_g, L0_attn_b_g,
           L0_attn_W_o, L0_attn_b_o, L0_ffn_Wfc_s, L0_ffn_bfc_s, L0_ffn_Wproj_s, L0_ffn_bproj_s, L0_ffn_Wr,
           L0_ffn_Wfc, L0_ffn_bfc, L0_ffn_Wproj, L0_ffn_bproj):
    import concourse.bacc as bacc
    from concourse.bass_utils import run_bass_kernel_spmd

    g, kind, j, copy, d = np.ix_(range(QT), range(2), range(4), range(4), range(KD))
    spread = (kind * P + (4 * g + j) * KD + d + 0 * copy).reshape(-1)
    shape = np.shape(L0_attn_x)
    arrays = {
        "x": np.reshape(L0_attn_x, (-1, P)),
        "const": constants(),
        "mask": decay_mask(),
        "w_qk": np.asarray(L0_attn_W_qk)[:, spread],
        "b_qk": np.asarray(L0_attn_b_qk)[spread].reshape(2 * QT, P).T,
        "w_vg": np.concatenate([L0_attn_W_v, L0_attn_W_g], axis=1),
        "b_vg": np.concatenate([L0_attn_b_v, L0_attn_b_g]),
        "w_o": L0_attn_W_o,
        "b_o": L0_attn_b_o,
        "wfc_s": L0_ffn_Wfc_s,
        "wproj_s": L0_ffn_Wproj_s,
        "wr": L0_ffn_Wr,
        "wfc": L0_ffn_Wfc,
        "wproj": L0_ffn_Wproj,
        "b_up": np.concatenate([np.reshape(L0_ffn_bfc_s, (1, HID)), L0_ffn_bfc]).reshape(EX * CH, P).T,
        "b_down": np.concatenate([L0_ffn_bproj, np.reshape(L0_ffn_bproj_s, (1, P))]),
    }
    nc = bacc.Bacc("TRN2", target_bir_lowering=False, num_devices=1)
    feeds, args = {}, []
    for name, a in arrays.items():
        a = np.ascontiguousarray(a)
        feeds[f"in_{name}"] = a
        args.append(nc.dram_tensor(f"in_{name}", a.shape, mybir.dt.from_np(a.dtype), kind="ExternalInput").ap())
    args.append(nc.dram_tensor("gate_scratch", (NE, TOK), F32).ap())
    args.append(nc.dram_tensor("out", feeds["in_x"].shape, F32, kind="ExternalOutput").ap())
    build(nc, *args)
    result = run_bass_kernel_spmd(nc, [feeds], core_ids=[0])
    return np.reshape(result.results[0]["out"], shape)
```

```python
from contextlib import ExitStack

import numpy as np
import concourse.bass as bass
from concourse import mybir

F32 = mybir.dt.float32
F32R = mybir.dt.float32r
U32 = mybir.dt.uint32
ALU = mybir.AluOpType
ACT = mybir.ActivationFunctionType
AX = mybir.AxisListType
ds = bass.ds

P = 128
SEQ = 256
HEADS, KD, VD = 16, 8, 16
VB = HEADS * VD
HID = 512
NE = 8
EX = NE + 1
TOK = 512
SUB = TOK // P
CH = HID // P
LN_EPS = 1e-5
RMS_EPS = float(np.finfo(np.float32).eps)
DENOM_LO, DENOM_HI = 1.0, 50000.0
H_RING, HL_RING, UP_RING, Y_RING, T_RING = 3, 6, 3, 3, 2
CAUSAL = 3 * P
C_ID, C_IOTA, C_QLOW, C_KLOW, C_END = 0, P, P + NE, P + NE + 1, P + NE + 2


def ffn_phase(nc, m, name, load, store):
    tiles = m["tokens"] // TOK
    ctx = ExitStack()
    with ctx:
        def sb(n, shape, dt=F32):
            return ctx.enter_context(nc.sbuf_tensor(f"{name}_{n}", shape, dt))

        def pb(n):
            return ctx.enter_context(nc.psum_tensor(f"{name}_{n}", [P, 512], F32))

        def sem(n):
            return ctx.enter_context(nc.semaphore(f"{name}_{n}"))

        x, w_hi, w_lo, const = m["x"], m["w_hi"], m["w_lo"], m["const"]
        wr, b_up, b_down = sb("wr", [P, NE]), sb("b_up", [P, EX * CH]), sb("b_down", [EX, P])
        ident = const[:, C_ID:C_ID + P]
        h = [sb(f"h{i}", [P, 2 * TOK]) for i in range(H_RING)]
        h_hi = [sb(f"h_hi{i}", [P, 2 * TOK], F32R) for i in range(HL_RING)]
        h_lo = [sb(f"h_lo{i}", [P, 2 * TOK], F32R) for i in range(HL_RING)]
        gate_bc = sb("gate_bc", [P, NE, TOK])
        xn = sb("xn", [P, SUB, P])
        xf = sb("xf", [P, TOK])
        x_hi = sb("x_hi", [P, TOK], F32R)
        x_lo = sb("x_lo", [P, TOK], F32R)
        acc = sb("acc", [P, TOK])
        gated = [sb(f"gated{i}", [P, TOK]) for i in range(T_RING)]
        gate_t = sb("gate_t", [EX, TOK])
        stats = sb("stats", [P, SUB, 6])
        mv = sb("mv", [P, SUB, 2])
        veps = sb("veps", [P, SUB])
        rstd = sb("rstd", [P, SUB])
        eps = sb("eps", [P, SUB])
        carrier = sb("carrier", [P, 1])
        half_neg = sb("half_neg", [P, SUB])
        euler = sb("euler", [P, SUB])
        logits = sb("logits", [P, SUB, NE])
        top = sb("top", [P, SUB, 8])
        topi = sb("topi", [P, SUB, 8], U32)
        gap = sb("gap", [P, SUB])
        egap = sb("egap", [P, SUB])
        egap1 = sb("egap1", [P, SUB])
        g1 = sb("g1", [P, SUB])
        g2 = sb("g2", [P, SUB])
        eq1 = sb("eq1", [P, SUB, NE])
        eq2 = sb("eq2", [P, SUB, NE])
        gate = sb("gate", [P, SUB, EX])
        stage = [sb(f"stage{i}", [P, 2 * HID]) for i in range(2)] if load else None

        up_ps = [pb(f"up{i}") for i in range(UP_RING)]
        y_ps = [pb(f"y{i}") for i in range(Y_RING)]
        t_ps = pb("t")
        r_ps = pb("r")

        loaded_x0, loaded_x1, loaded_x = sem("loaded_x0"), sem("loaded_x1"), sem("loaded_x")
        loaded_small, loaded_const = sem("loaded_small"), sem("loaded_const")
        loaded_w = [sem(f"loaded_w{e}") for e in range(EX)] if load else None
        w_hi_done, w_lo_done = sem("w_hi_done"), sem("w_lo_done")
        stored = sem("stored")
        preset = sem("preset")
        up_done, gelu_done, hi_done, lo_done = sem("up_done"), sem("gelu_done"), sem("hi_done"), sem("lo_done")
        down_done, y_taken, acc_added = sem("down_done"), sem("y_taken"), sem("acc_added")
        acc_turned, x_updated = sem("acc_turned"), sem("x_updated")
        stats_step, var_eps, rstd_done, xn_done = sem("stats_step"), sem("var_eps"), sem("rstd_done"), sem("xn_done")
        xn_turned, xf_done, xs_hi, xs_done = sem("xn_turned"), sem("xf_done"), sem("xs_hi"), sem("xs_done")
        logits_done, router_step, egap_done = sem("logits_done"), sem("router_step"), sem("egap_done")
        gate_turned, gate_t_done = sem("gate_turned"), sem("gate_t_done")
        gates_out, gates_a, gates_b = sem("gates_out"), sem("gates_b1"), sem("gates_b2")
        STATS = 2 * SUB
        ROUTER = 7 + 2 * SUB
        block = ctx.enter_context(nc.Block())

        def first(t):
            return isinstance(t, int) and t == 0

        @block.sync
        def _(sp):
            def spread_gates(t):
                sp.wait_ge(gate_t_done, t + 1)
                if not first(t):
                    sp.wait_ge(gates_a, 16 * t)
                    sp.wait_ge(gates_b, 16 * t)
                sp.dma_start(m["gate_dram"], gate_t[0:NE, :]).then_inc(gates_out, 16)
                sp.wait_ge(gates_out, 16 * (t + 1))
                half = NE // 2
                if not first(t):
                    sp.wait_ge(y_taken, EX * (t - 1) + half + 1)
                sp.dma_start(gate_bc[:, 0:half, :], m["gate_dram"][0:half, :].partition_broadcast(P)).then_inc(gates_a, 16)
                if not first(t):
                    sp.wait_ge(y_taken, EX * t)
                sp.dma_start(gate_bc[:, half:, :], m["gate_dram"][half:, :].partition_broadcast(P)).then_inc(gates_b, 16)

            def store_x(t):
                sp.wait_ge(x_updated, t + 1)
                sp.dma_start(m["out_dram"][:, ds(SUB * t, SUB), :], x[:, ds(SUB * t, SUB), :]).then_inc(stored, 16)

            if load:
                sp.dma_start(x[:, 0:SUB, :], m["x_dram"][:, 0:SUB, :]).then_inc(loaded_x0, 16)
                sp.dma_start(const[:], m["const_dram"]).then_inc(loaded_const, 16)
            for dst, src in ((wr[:], m["wr_dram"]), (b_up[:], m["b_up_dram"]), (b_down[:], m["b_down_dram"])):
                sp.dma_start(dst, src).then_inc(loaded_small, 16)
            if load:
                for e in range(EX):
                    if e >= 2:
                        sp.wait_ge(w_lo_done, e - 1)
                    up, down = m["w_dram"][e]
                    sp.dma_start(stage[e % 2][:, 0:HID], up).then_inc(loaded_w[e], 16)
                    sp.dma_start(stage[e % 2][:, HID:].rearrange("p (c n) -> p c n", c=CH), down)\
                      .then_inc(loaded_w[e], 16)
                    if e == 0:
                        sp.dma_start(x[:, SUB:2 * SUB, :], m["x_dram"][:, SUB:2 * SUB, :]).then_inc(loaded_x1, 16)
                    if e == 2:
                        spread_gates(0)
                sp.dma_start(x[:, 2 * SUB:, :], m["x_dram"][:, 2 * SUB:, :]).then_inc(loaded_x, 16)
            else:
                spread_gates(0)

            def tile(t):
                spread_gates(t + 1)
                if store:
                    store_x(t)

            tile(0)
            with sp.Fori(1, tiles - 1) as t:
                tile(t)
            if store:
                store_x(tiles - 1)
                sp.wait_ge(stored, 16 * tiles)
            sp.wait_ge(gates_out, 16 * tiles)

        @block.tensor
        def _(pe):
            def prep_turn(t):
                pe.wait_ge(xn_done, SUB * (t + 1))
                if not isinstance(t, int) or t > 1:
                    pe.wait_ge(x_updated, t - 1)
                for j in range(SUB):
                    last = pe.transpose(t_ps[:, j * P:(j + 1) * P], xn[:, j, :], ident)
                last.then_inc(xn_turned, 1)

            def prep_logits(t):
                pe.wait_ge(xf_done, t + 1)
                if not first(t):
                    pe.wait_ge(gate_t_done, t)
                for j in range(SUB):
                    last = pe.matmul(r_ps[:, j * NE:(j + 1) * NE], xf[:, j * P:(j + 1) * P], wr[:],
                                     start=True, stop=True)
                last.then_inc(logits_done, 1)

            def prep_gates(t):
                pe.wait_ge(router_step, ROUTER * (t + 1))
                for j in range(SUB):
                    last = pe.transpose(r_ps[0:EX, j * P:(j + 1) * P], gate[:, j, :], ident)
                last.then_inc(gate_turned, 1)

            def up(t, e):
                if e == 0:
                    pe.wait_ge(xs_done, t + 1)
                if load and first(t):
                    pe.wait_ge(w_lo_done, e + 1)
                for c in range(CH):
                    q = CH * e + c
                    if not first(t) or q >= UP_RING:
                        pe.wait_ge(gelu_done, EX * CH * t + q - UP_RING + 1)
                    bank = up_ps[q % UP_RING]
                    hi, lo = w_hi[:, e, c * P:(c + 1) * P], w_lo[:, e, c * P:(c + 1) * P]
                    pe.matmul(bank[:], hi, x_hi[:], start=True, stop=False)
                    pe.matmul(bank[:], hi, x_lo[:], start=False, stop=False)
                    pe.matmul(bank[:], lo, x_hi[:], start=False, stop=True).then_inc(up_done, 1)

            def down(t, e):
                bank = y_ps[e % Y_RING]
                if not first(t) or e >= Y_RING:
                    pe.wait_ge(y_taken, EX * t + e - Y_RING + 1)
                if e == 0:
                    pe.wait_ge(gate_t_done, t + 1)
                    pe.matmul(bank[:], b_down[:], gate_t[:], start=True, stop=False)
                for c in range(CH):
                    half = 2 * e + c // 2
                    if c % 2 == 0:
                        pe.wait_ge(lo_done, 2 * EX * t + half + 1)
                    cols = slice((c % 2) * TOK, (c % 2 + 1) * TOK)
                    hi = w_hi[:, e, HID + c * P:HID + (c + 1) * P]
                    lo = w_lo[:, e, HID + c * P:HID + (c + 1) * P]
                    a_hi, a_lo = h_hi[half % HL_RING][:, cols], h_lo[half % HL_RING][:, cols]
                    pe.matmul(bank[:], hi, a_hi, start=(c == 0 and e > 0), stop=False)
                    pe.matmul(bank[:], hi, a_lo, start=False, stop=False)
                    last = pe.matmul(bank[:], lo, a_hi, start=False, stop=(c == CH - 1))
                last.then_inc(down_done, 1)

            def turn_back(t):
                pe.wait_ge(acc_added, NE * (t + 1))
                if is_last(t):
                    pe.wait_ge(x_updated, t)
                else:
                    pe.wait_ge(xf_done, t + 2)
                for j in range(SUB):
                    last = pe.transpose(t_ps[:, j * P:(j + 1) * P], acc[:, j * P:(j + 1) * P], ident)
                last.then_inc(acc_turned, 1)

            def is_last(t):
                return isinstance(t, int) and t == tiles - 1

            def tile(t, prep=True):
                for e in range(EX):
                    up(t, e)
                    if e:
                        down(t, e - 1)
                    elif not first(t):
                        down(t - 1, EX - 1)
                    if e == 1 and not first(t):
                        turn_back(t - 1)
                    if prep:
                        if e == 3:
                            prep_turn(t + 1)
                        if e == 4:
                            prep_logits(t + 1)
                        if e == 6:
                            prep_gates(t + 1)

            pe.wait_ge(preset, 1)
            pe.wait_ge(loaded_small, 48)
            if load:
                pe.wait_ge(loaded_const, 16)
            prep_turn(0)
            prep_logits(0)
            prep_gates(0)
            tile(0)
            with pe.Fori(1, tiles - 1) as t:
                tile(t)
            tile(tiles - 1, prep=False)
            down(tiles - 1, EX - 1)
            turn_back(tiles - 1)

        @block.scalar
        def _(act):
            def prep_take(t):
                act.wait_ge(xn_turned, t + 1)
                if not first(t):
                    act.wait_ge(xs_done, t)
                    act.wait_ge(logits_done, t)
                act.activation(xf[:], t_ps[:], ACT.Copy).then_inc(xf_done, 1)

            def prep_gates(t):
                act.wait_ge(gate_turned, t + 1)
                if not first(t):
                    act.wait_ge(gates_out, 16 * t)
                    act.wait_ge(down_done, EX * (t - 1) + 1)
                act.activation(gate_t[:], r_ps[0:EX, :], ACT.Copy).then_inc(gate_t_done, 1)

            def split_weights(e):
                act.wait_ge(loaded_w[e], 32)
                act.activation(w_hi[:, e, :], stage[e % 2][:], ACT.Copy).then_inc(w_hi_done, 1)

            def tile(t, prep=True):
                for e in range(EX):
                    if prep:
                        if e == 4:
                            prep_take(t + 1)
                        if e == 7:
                            prep_gates(t + 1)
                    for s in range(2):
                        half = 2 * e + s
                        buf = h[half % H_RING]
                        if not first(t) or half >= H_RING:
                            act.wait_ge(lo_done, 2 * EX * t + half - H_RING + 1)
                        for k in range(2):
                            q = 2 * half + k
                            act.wait_ge(up_done, EX * CH * t + q + 1)
                            act.activation(buf[:, k * TOK:(k + 1) * TOK], up_ps[q % UP_RING][:],
                                           ACT.Gelu_apprx_tanh, bias=b_up[:, CH * e + q % CH:CH * e + q % CH + 1])\
                               .then_inc(gelu_done, 1)
                        act.wait_ge(gelu_done, EX * CH * t + 2 * half + 2)
                        if not first(t) or half >= HL_RING:
                            act.wait_ge(down_done, EX * t + e - HL_RING // 2 + 1)
                        act.activation(h_hi[half % HL_RING][:], buf[:], ACT.Copy).then_inc(hi_done, 1)
                    if load and first(t) and e + 1 < EX:
                        split_weights(e + 1)

            act.wait_ge(loaded_small, 48)
            if load:
                split_weights(0)
            prep_take(0)
            prep_gates(0)
            tile(0)
            with act.Fori(1, tiles - 1) as t:
                tile(t)
            tile(tiles - 1, prep=False)

        @block.vector
        def _(dve):
            def prep_stats(t):
                if load:
                    if isinstance(t, int) and t < 2:
                        dve.wait_ge((loaded_x0, loaded_x1)[t], 16)
                    else:
                        dve.wait_ge(loaded_x, 16)
                if not first(t):
                    dve.wait_ge(rstd_done, t)
                    dve.wait_ge(xn_done, SUB * t)
                for j in range(SUB):
                    dve.bn_stats(stats[:, j, :], x[:, ds(SUB * t + j, 1), :].squeeze(1)).then_inc(stats_step, 1)
                dve.wait_ge(stats_step, STATS * t + SUB)
                dve.memset(carrier[:], 0.0)
                for j in range(SUB):
                    dve.bn_aggr(mv[:, j, :], stats[:, j, :]).then_inc(stats_step, 1)

            def prep_normalise(t):
                dve.wait_ge(rstd_done, t + 1)
                dve.wait_ge(stats_step, STATS * (t + 1))
                if not first(t):
                    dve.wait_ge(xn_turned, t)
                for j in range(SUB):
                    dve.tensor_scalar(xn[:, j, :], x[:, ds(SUB * t + j, 1), :].squeeze(1), mv[:, j, 0:1],
                                      rstd[:, j:j + 1], ALU.subtract, ALU.mult).then_inc(xn_done, 1)

            def prep_split(t):
                dve.wait_ge(xf_done, t + 1)
                if not first(t):
                    dve.wait_ge(up_done, EX * CH * t)
                dve.tensor_copy(x_hi[:], xf[:]).then_inc(xs_hi, 1)
                dve.wait_ge(xs_hi, t + 1)
                dve.tensor_tensor(x_lo[:], xf[:], x_hi[:].bitcast(F32), ALU.subtract).then_inc(xs_done, 1)

            def router_top(t):
                base = ROUTER * t
                dve.wait_ge(logits_done, t + 1)
                if not first(t):
                    dve.wait_ge(router_step, base)
                dve.tensor_copy(logits[:].rearrange("p j e -> p (j e)"), r_ps[:, 0:SUB * NE]).then_inc(router_step, 1)
                dve.wait_ge(router_step, base + 1)
                dve.memset(carrier[:], 0.0)
                for j in range(SUB):
                    dve.max(top[:, j, :], logits[:, j, :]).then_inc(router_step, 1)
                dve.wait_ge(router_step, base + 1 + SUB)
                dve.memset(carrier[:], 0.0)
                for j in range(SUB):
                    dve.max_index(topi[:, j, :], top[:, j, :], logits[:, j, :]).then_inc(router_step, 1)
                dve.tensor_tensor(gap[:], top[:, :, 1], top[:, :, 0], ALU.subtract).then_inc(router_step, 1)

            def router_gates(t):
                base = ROUTER * t + 2 + 2 * SUB
                wide = [P, SUB, NE]
                iota = const[:, C_IOTA:C_IOTA + NE].unsqueeze(1).to_broadcast(wide)
                dve.wait_ge(egap_done, t + 1)
                if not first(t):
                    dve.wait_ge(gate_turned, t)
                dve.wait_ge(router_step, base)
                dve.tensor_tensor(eq1[:], topi[:, :, 0:1].to_broadcast(wide), iota, ALU.is_equal)
                dve.tensor_tensor(eq2[:], topi[:, :, 1:2].to_broadcast(wide), iota, ALU.is_equal)
                dve.tensor_scalar(egap1[:], egap[:], 1.0, None, ALU.add).then_inc(router_step, 1)
                dve.wait_ge(router_step, base + 1)
                dve.reciprocal(g1[:], egap1[:]).then_inc(router_step, 1)
                dve.wait_ge(router_step, base + 2)
                dve.tensor_tensor(g2[:], egap[:], g1[:], ALU.mult)
                dve.tensor_tensor(eq1[:], eq1[:], g1[:].unsqueeze(2).to_broadcast(wide), ALU.mult).then_inc(router_step, 1)
                dve.wait_ge(router_step, base + 3)
                dve.tensor_tensor(eq2[:], eq2[:], g2[:].unsqueeze(2).to_broadcast(wide), ALU.mult).then_inc(router_step, 1)
                dve.wait_ge(router_step, base + 4)
                dve.tensor_tensor(gate[:, :, 0:NE], eq1[:], eq2[:], ALU.add).then_inc(router_step, 1)

            def lo(t, half):
                dve.wait_ge(hi_done, 2 * EX * t + half + 1)
                if not first(t) or half >= HL_RING:
                    dve.wait_ge(down_done, EX * t + half // 2 - HL_RING // 2 + 1)
                dve.tensor_tensor(h_lo[half % HL_RING][:], h[half % H_RING][:],
                                  h_hi[half % HL_RING][:].bitcast(F32), ALU.subtract).then_inc(lo_done, 1)

            def take(t, e):
                dve.wait_ge(down_done, EX * t + e + 1)
                if e == 0:
                    if not first(t):
                        dve.wait_ge(acc_turned, t)
                    dve.tensor_copy(acc[:], y_ps[0][:]).then_inc(y_taken, 1)
                    return
                if e == 1:
                    dve.wait_ge(gates_a, 16 * (t + 1))
                if e == NE // 2 + 1:
                    dve.wait_ge(gates_b, 16 * (t + 1))
                if not first(t) or e > T_RING:
                    dve.wait_ge(acc_added, NE * t + e - T_RING)
                dve.tensor_tensor(gated[e % T_RING][:], y_ps[e % Y_RING][:], gate_bc[:, e - 1, :], ALU.mult)\
                   .then_inc(y_taken, 1)

            def update(t):
                dve.wait_ge(acc_turned, t + 1)
                rows = x[:, ds(SUB * t, SUB), :].rearrange("p j c -> p (j c)")
                dve.scalar_tensor_tensor(rows, t_ps[:], 0.5, rows, ALU.mult, ALU.add).then_inc(x_updated, 1)

            def split_weights(e):
                dve.wait_ge(w_hi_done, e + 1)
                dve.tensor_tensor(w_lo[:, e, :], stage[e % 2][:], w_hi[:, e, :].bitcast(F32), ALU.subtract)\
                   .then_inc(w_lo_done, 1)

            def tile(t, prep=True):
                for e in range(EX):
                    lo(t, 2 * e)
                    if prep and e == EX - 1:
                        prep_split(t + 1)
                    lo(t, 2 * e + 1)
                    if load and first(t) and e + 1 < EX:
                        split_weights(e + 1)
                    if e:
                        take(t, e - 1)
                    elif not first(t):
                        take(t - 1, EX - 1)
                    if e == 2 and not first(t):
                        update(t - 1)
                    if prep:
                        if e == 1:
                            prep_stats(t + 1)
                        if e == 2:
                            prep_normalise(t + 1)
                        if e == 4:
                            router_top(t + 1)
                        if e == 5:
                            router_gates(t + 1)

            dve.memset(half_neg[:], -0.5)
            dve.memset(eps[:], LN_EPS)
            dve.memset(euler[:], float(np.e))
            dve.memset(gate[:, :, NE:EX], 1.0).then_inc(preset, 1)
            if load:
                dve.wait_ge(loaded_const, 16)
            prep_stats(0)
            prep_normalise(0)
            if load:
                split_weights(0)
            router_top(0)
            prep_split(0)
            router_gates(0)
            tile(0)
            with dve.Fori(1, tiles - 1) as t:
                tile(t)
            tile(tiles - 1, prep=False)
            take(tiles - 1, EX - 1)
            update(tiles - 1)

        @block.gpsimd
        def _(pool):
            def prep_rstd(t):
                pool.wait_ge(stats_step, STATS * (t + 1))
                if not first(t):
                    pool.wait_ge(xn_done, SUB * t)
                pool.tensor_tensor(veps[:], mv[:, :, 1], eps[:], ALU.add).then_inc(var_eps, 1)
                pool.wait_ge(var_eps, t + 1)
                pool.tensor_tensor(rstd[:], veps[:], half_neg[:], ALU.pow).then_inc(rstd_done, 1)

            def router_exp(t):
                pool.wait_ge(router_step, ROUTER * t + 2 + 2 * SUB)
                pool.tensor_tensor(egap[:], euler[:], gap[:], ALU.pow).then_inc(egap_done, 1)

            def add(t, e):
                pool.wait_ge(y_taken, EX * t + e + 1)
                if not first(t) or e > 1:
                    pool.wait_ge(acc_added, NE * t + e - 1)
                pool.tensor_tensor(acc[:], acc[:], gated[e % T_RING][:], ALU.add).then_inc(acc_added, 1)

            def tile(t, prep=True):
                for e in range(EX):
                    if e >= 2:
                        add(t, e - 1)
                    elif e == 0 and not first(t):
                        add(t - 1, EX - 1)
                    if prep:
                        if e == 1:
                            prep_rstd(t + 1)
                        if e == 4:
                            router_exp(t + 1)

            pool.wait_ge(preset, 1)
            prep_rstd(0)
            router_exp(0)
            tile(0)
            with pool.Fori(1, tiles - 1) as t:
                tile(t)
            tile(tiles - 1, prep=False)
            add(tiles - 1, EX - 1)

PAIRS = HEADS // 2
QT = 4
S_RING, M_RING, A_RING, F_RING = 2, 3, 3, 2


def retention_phase(nc, m):
    seqs = m["tokens"] // SEQ
    TB = SEQ // P
    ctx = ExitStack()
    with ctx:
        def sb(n, shape, dt=F32):
            return ctx.enter_context(nc.sbuf_tensor(f"ret_{n}", shape, dt))

        def pb(n, shape):
            return ctx.enter_context(nc.psum_tensor(f"ret_{n}", shape, F32))

        def sem(n):
            return ctx.enter_context(nc.semaphore(f"ret_{n}"))

        x, const = m["x"], m["const"]
        ident = const[:, C_ID:C_ID + P]
        mask = sb("mask", [P, HEADS, CAUSAL])
        wqk_hi = sb("wqk_hi", [P, 2 * QT * P], F32R)
        wqk_lo = sb("wqk_lo", [P, 2 * QT * P], F32R)
        wvg_hi = sb("wvg_hi", [P, 2 * VB], F32R)
        wvg_lo = sb("wvg_lo", [P, 2 * VB], F32R)
        wo = sb("wo", [P, VB // P, P])
        bqk = sb("bqk", [P, 2 * QT])
        bvg = sb("bvg", [P, 2 * VB])
        bo = sb("bo", [P, P])
        f = [sb(f"f{i}", [P, 2, SEQ]) for i in range(F_RING)]
        qk = [sb(f"qk{i}", [P, 2 * QT, SEQ], F32R) for i in range(2)]
        v = [sb(f"v{i}", [P, TB, PAIRS, 3, VD]) for i in range(2)]
        gates = [sb(f"gates{i}", [P, TB, VB]) for i in range(2)]
        masked = [sb(f"masked{i}", [P, 2, CAUSAL]) for i in range(M_RING)]
        absed = [sb(f"absed{i}", [P, 2, CAUSAL]) for i in range(A_RING)]
        pick = sb("pick", [P, 32 + HEADS // 4 - 1])
        sums = sb("sums", [P, SEQ])
        xn = sb("xn", [P, TB, P])
        x_hi = sb("x_hi", [P, SEQ], F32R)
        x_lo = sb("x_lo", [P, SEQ], F32R)
        stats = sb("stats", [P, TB, 6])
        mv = sb("mv", [P, TB, 2])
        veps = sb("veps", [P, TB])
        rstd = sb("rstd", [P, TB])
        eps = sb("eps", [P, TB])
        carrier = sb("carrier", [P, 1])
        half_neg = sb("half_neg", [P, TB])
        r_turned = sb("r_turned", [P, TB * VB])
        r_sb = sb("r_sb", [P, TB * VB])
        square = sb("square", [P, TB * VB])
        denom = sb("denom", [P, TB * HEADS])
        ssum = sb("ssum", [P, TB * HEADS])
        gated_t = square

        w_qk = mask[:].rearrange("p h c -> p (h c)")[:, 0:2 * QT * P]
        w_vg = mask[:].rearrange("p h c -> p (h c)")[:, 2 * QT * P:2 * QT * P + 2 * VB]

        s_ps = pb("s", [P, S_RING, 2, 512])
        r_ps = pb("r", [P, TB * VB])
        a_ps = pb("a", [P, 512])
        t_ps = pb("t", [P, 512])
        p_ps = pb("p", [P, 2, SEQ])

        loaded, loaded_mask = sem("loaded"), sem("loaded_mask")
        split_hi, split_lo, preset = sem("split_hi"), sem("split_lo"), sem("preset")
        stats_step, var_eps, rstd_done, xn_done = sem("stats_step"), sem("var_eps"), sem("rstd_done"), sem("xn_done")
        bias_added = sem("bias_added")
        xn_turned, x_hi_done, x_lo_done = sem("xn_turned"), sem("x_hi_done"), sem("x_lo_done")
        projected, f_done, qk_done, vg_done = sem("projected"), sem("f_done"), sem("qk_done"), sem("vg_done")
        scored, mask_done, mixed = sem("scored"), sem("mask_done"), sem("mixed")
        abs_done, summed = sem("abs_done"), sem("summed")
        sums_taken, sums_turned = sem("sums_taken"), sem("sums_turned")
        r_evicted, r_back, r_taken, square_done = sem("r_evicted"), sem("r_back"), sem("r_taken"), sem("square_done")
        norm_step, root_done, r_gated, norm_applied = sem("norm_step"), sem("root_done"), sem("r_gated"), sem("norm_applied")
        gated_turned, gated_t_done, out_done, x_updated = sem("gated_turned"), sem("gated_t_done"), sem("out_done"), sem("x_updated")
        STATS, NORM = 2 * TB, 5
        VG_ITEMS = TB
        ITEMS = QT + VG_ITEMS
        block = ctx.enter_context(nc.Block())

        def first(b):
            return isinstance(b, int) and b == 0

        def last_use(p, ring):
            return p - ring if p >= ring else max(q for q in range(PAIRS) if q % ring == p) - PAIRS

        @block.sync
        def _(sp):
            for dst, src in ((w_qk, m["w_qk_dram"]), (w_vg, m["w_vg_dram"]), (wo[:], m["w_o_dram"]), (bqk[:], m["b_qk_dram"]),
                             (bvg[:], m["b_vg_dram"].partition_broadcast(P)),
                             (bo[:], m["b_o_dram"].partition_broadcast(P))):
                sp.dma_start(dst, src).then_inc(loaded, 16)
            sp.wait_ge(split_lo, 2)
            sp.dma_start(mask[:], m["mask_dram"]).then_inc(loaded_mask, 16)

        @block.tensor
        def _(pe):
            def turn(b):
                pe.wait_ge(xn_done, TB * (b + 1))
                if not isinstance(b, int) or b > 2:
                    pe.wait_ge(norm_step, NORM * (b - 3) + 1)
                for j in range(TB):
                    last = pe.transpose(t_ps[:, j * P:(j + 1) * P], xn[:, j, :], ident)
                last.then_inc(xn_turned, 1)

            def project_qk(b, g):
                if g == 0:
                    pe.wait_ge(x_lo_done, b + 1)
                if not first(b) or g:
                    wait_bank(b, g)
                for k in range(2):
                    cols = slice((2 * g + k) * P, (2 * g + k + 1) * P)
                    pe.matmul(p_ps[:, k, :], wqk_hi[:, cols], x_hi[:], start=True, stop=False)
                    pe.matmul(p_ps[:, k, :], wqk_hi[:, cols], x_lo[:], start=False, stop=False)
                    last = pe.matmul(p_ps[:, k, :], wqk_lo[:, cols], x_hi[:], start=False, stop=True)
                last.then_inc(projected, 1)

            def project_vg(b, j):
                wait_bank(b, QT + j)
                out = p_ps[:].rearrange("p a b -> p (a b)")
                hi, lo = x_hi[:, j * P:(j + 1) * P], x_lo[:, j * P:(j + 1) * P]
                pe.matmul(out, hi, wvg_hi[:], start=True, stop=False)
                pe.matmul(out, hi, wvg_lo[:], start=False, stop=False)
                pe.matmul(out, lo, wvg_hi[:], start=False, stop=True).then_inc(projected, 1)

            def wait_bank(b, item):
                if item == 0:
                    pe.wait_ge(vg_done, VG_ITEMS * b)
                elif item <= QT:
                    pe.wait_ge(f_done, 2 * (QT * b + item))
                else:
                    pe.wait_ge(vg_done, VG_ITEMS * b + item - QT)

            def scores(b, par, p):
                pe.wait_ge(qk_done, QT * b + p // 2 + 1)
                if not first(b) or p >= S_RING:
                    pe.wait_ge(mask_done, PAIRS * b + p - S_RING + 1)
                for i in range(2):
                    g, j = (2 * p + i) // 4, (2 * p + i) % 4
                    rows = slice(32 * j, 32 * j + 32)
                    q, k = qk[par][rows, 2 * g, :], qk[par][rows, 2 * g + 1, :]
                    pe.matmul(s_ps[:, p % S_RING, i, 0:SEQ], k[:, P:SEQ], q, start=True, stop=True)
                    last = pe.matmul(s_ps[:, p % S_RING, i, SEQ:2 * SEQ], k[:, 0:P], q, start=True, stop=True)
                last.then_inc(scored, 1)

            def mix(b, par, p):
                pe.wait_ge(mask_done, PAIRS * b + p + 1)
                if p == 0:
                    pe.wait_ge(vg_done, VG_ITEMS * (b + 1))
                    if not first(b):
                        pe.wait_ge(r_evicted, b)
                rows, base = slice(32 * (p % 4), 32 * (p % 4) + 32), p // 4 * SEQ
                for i in range(2):
                    v0, v1 = (v[par][:, j, p, i:i + 2, :].rearrange("p a d -> p (a d)") for j in range(TB))
                    src = masked[p % M_RING]
                    pe.matmul(r_ps[rows, base:base + SEQ], v0, src[:, i, P:3 * P], start=(i == 0), stop=False)
                    last = pe.matmul(r_ps[rows, base + P:base + SEQ], v1, src[:, i, 0:P], start=False, stop=(i == 1))
                last.then_inc(mixed, 1)

            def add_up(b, p):
                pe.wait_ge(abs_done, PAIRS * b + p + 1)
                if p == 0 and not first(b):
                    pe.wait_ge(sums_taken, b)
                for i in range(2):
                    h = 2 * p + i
                    rows, r = slice(32 * (h % 4), 32 * (h % 4) + 32), h // 4
                    one, src = pick[:, HEADS // 4 - 1 - r:HEADS // 4 - 1 - r + 32], absed[p % A_RING]
                    pe.matmul(a_ps[rows, 0:SEQ], one, src[:, i, P:CAUSAL], start=(r == 0), stop=False)
                    last = pe.matmul(a_ps[rows, P:SEQ], one, src[:, i, 0:P], start=False, stop=(r == HEADS // 4 - 1))
                last.then_inc(summed, 1)

            def turn_r(b):
                pe.wait_ge(r_evicted, b + 1)
                if first(b):
                    pe.wait_ge(x_lo_done, 3)
                else:
                    pe.wait_ge(x_updated, b)
                for j in range(TB):
                    for k in range(VB // P):
                        last = pe.transpose(t_ps[:, j * VB + k * P:j * VB + (k + 1) * P],
                                            r_turned[:, k * SEQ + j * P:k * SEQ + (j + 1) * P], ident)
                last.then_inc(r_back, 1)

            def turn_sums(b):
                pe.wait_ge(sums_taken, b + 1)
                pe.wait_ge(square_done, b + 1)
                for j in range(TB):
                    last = pe.transpose(t_ps[:, j * P:(j + 1) * P], sums[:, j * P:(j + 1) * P], ident)
                last.then_inc(sums_turned, 1)

            def turn_gated(b):
                pe.wait_ge(norm_applied, b + 1)
                if not isinstance(b, int) or b < seqs - 3:
                    pe.wait_ge(x_lo_done, b + 4)
                for j in range(TB):
                    for k in range(VB // P):
                        last = pe.transpose(t_ps[:, k * SEQ + j * P:k * SEQ + (j + 1) * P],
                                            r_sb[:, j * VB + k * P:j * VB + (k + 1) * P], ident)
                last.then_inc(gated_turned, 1)

            def project_out(b):
                pe.wait_ge(gated_t_done, b + 1)
                for j in range(TB):
                    for k in range(VB // P):
                        last = pe.matmul(t_ps[:, j * P:(j + 1) * P], gated_t[:, k * SEQ + j * P:k * SEQ + (j + 1) * P],
                                         wo[:, k, :], start=(k == 0), stop=(k == VB // P - 1))
                last.then_inc(out_done, 1)

            def sequence(b, par, prep=True):
                for p in range(PAIRS):
                    if p:
                        mix(b, par, p - 1)
                    elif not first(b):
                        mix(b - 1, 1 - par, PAIRS - 1)
                    if prep and p == 0:
                        turn(b + 1)
                    if p < PAIRS - 1:
                        scores(b, par, p + 1)
                    elif prep:
                        scores(b + 1, 1 - par, 0)
                    if p >= 2:
                        add_up(b, p - 2)
                    elif not first(b):
                        add_up(b - 1, PAIRS - 2 + p)
                    if not isinstance(b, int) or b > 1:
                        if p == 1:
                            turn_gated(b - 2)
                        if p == 2:
                            project_out(b - 2)
                    if not first(b):
                        if p == 4:
                            turn_r(b - 1)
                        if p == 5:
                            turn_sums(b - 1)
                    if prep:
                        if 0 < p <= QT:
                            project_qk(b + 1, p - 1)
                        elif QT < p <= ITEMS:
                            project_vg(b + 1, p - QT - 1)

            pe.wait_ge(preset, 3)
            pe.wait_ge(split_lo, 2)
            turn(0)
            for g in range(QT):
                project_qk(0, g)
            for j in range(TB):
                project_vg(0, j)
            scores(0, 0, 0)
            sequence(0, 0)
            sequence(1, 1)
            with pe.Fori(1, seqs // 2 - 1) as two:
                sequence(2 * two, 0)
                sequence(2 * two + 1, 1)
            sequence(seqs - 2, 0)
            sequence(seqs - 1, 1, prep=False)
            mix(seqs - 1, 1, PAIRS - 1)
            add_up(seqs - 1, PAIRS - 2)
            add_up(seqs - 1, PAIRS - 1)
            turn_gated(seqs - 2)
            project_out(seqs - 2)
            turn_r(seqs - 1)
            turn_sums(seqs - 1)
            turn_gated(seqs - 1)
            project_out(seqs - 1)

        @block.scalar
        def _(act):
            def take_x(b):
                act.wait_ge(xn_turned, b + 1)
                if not first(b):
                    act.wait_ge(projected, ITEMS * b)
                act.activation(x_hi[:], t_ps[:, 0:SEQ], ACT.Copy).then_inc(x_hi_done, 1)

            def take_qk(b, par, g):
                act.wait_ge(projected, ITEMS * b + g + 1)
                if not isinstance(b, int) or b > 1:
                    act.wait_ge(scored, PAIRS * (b - 1))
                for k in range(2):
                    act.activation(qk[par][:, 2 * g + k, :], p_ps[:, k, :], ACT.Identity,
                                   bias=bqk[:, 2 * g + k:2 * g + k + 1])
                if not first(b) or g >= F_RING:
                    act.wait_ge(qk_done, QT * b + g - F_RING + 1)
                for k in range(2):
                    act.activation(f[g % F_RING][:, k, :], p_ps[:, k, :], ACT.Identity,
                                   bias=bqk[:, 2 * g + k:2 * g + k + 1]).then_inc(f_done, 1)

            def magnitudes(b, p):
                act.wait_ge(mask_done, PAIRS * b + p + 1)
                if not first(b) or p >= A_RING:
                    act.wait_ge(summed, PAIRS * b + last_use(p, A_RING) + 1)
                act.activation(absed[p % A_RING][:], masked[p % M_RING][:], ACT.Abs).then_inc(abs_done, 1)

            def evict_r(b):
                act.wait_ge(mixed, PAIRS * (b + 1))
                if not first(b):
                    act.wait_ge(r_back, b)
                act.activation(r_turned[:], r_ps[:], ACT.Copy).then_inc(r_evicted, 1)

            def take_r(b):
                act.wait_ge(r_back, b + 1)
                if not first(b):
                    act.wait_ge(gated_turned, b)
                act.activation(r_sb[:], t_ps[:], ACT.Copy).then_inc(r_taken, 1)
                if not first(b):
                    act.wait_ge(out_done, b)
                act.activation(square[:], t_ps[:], ACT.Square).then_inc(square_done, 1)

            def take_sums(b):
                act.wait_ge(summed, PAIRS * (b + 1))
                if not first(b):
                    act.wait_ge(sums_turned, b)
                act.activation(sums[:], a_ps[:, 0:SEQ], ACT.Copy).then_inc(sums_taken, 1)

            def take_gated(b):
                act.wait_ge(gated_turned, b + 1)
                act.wait_ge(norm_step, NORM * (b + 1))
                act.activation(gated_t[:], t_ps[:], ACT.Copy).then_inc(gated_t_done, 1)

            def root(b):
                act.wait_ge(norm_step, NORM * b + 4)
                act.activation(ssum[:], ssum[:], ACT.Sqrt).then_inc(root_done, 1)

            def sequence(b, par, prep=True):
                for p in range(PAIRS):
                    if p == 0 and not first(b):
                        evict_r(b - 1)
                    if prep and p == 0:
                        take_x(b + 1)
                    if p == 2 and not first(b):
                        take_sums(b - 1)
                    if p == 2 and (not isinstance(b, int) or b > 1):
                        take_gated(b - 2)
                    if p == 5 and not first(b):
                        take_r(b - 1)
                    if prep and 2 <= p <= QT + 1:
                        take_qk(b + 1, 1 - par, p - 2)
                    if p == 7 and not first(b):
                        root(b - 1)
                    magnitudes(b, p)

            act.wait_ge(loaded, 96)
            act.activation(wqk_hi[:], w_qk, ACT.Copy).then_inc(split_hi, 1)
            act.activation(wvg_hi[:], w_vg, ACT.Copy).then_inc(split_hi, 1)
            take_x(0)
            for g in range(QT):
                take_qk(0, 0, g)
            sequence(0, 0)
            sequence(1, 1)
            with act.Fori(1, seqs // 2 - 1) as two:
                sequence(2 * two, 0)
                sequence(2 * two + 1, 1)
            sequence(seqs - 2, 0)
            sequence(seqs - 1, 1, prep=False)
            evict_r(seqs - 1)
            take_gated(seqs - 2)
            take_sums(seqs - 1)
            take_r(seqs - 1)
            root(seqs - 1)
            take_gated(seqs - 1)

        @block.vector
        def _(dve):
            def prep_stats(b):
                if not first(b):
                    dve.wait_ge(rstd_done, b)
                    dve.wait_ge(xn_done, TB * b)
                for j in range(TB):
                    dve.bn_stats(stats[:, j, :], x[:, ds(TB * b + j, 1), :].squeeze(1)).then_inc(stats_step, 1)
                dve.wait_ge(stats_step, STATS * b + TB)
                dve.memset(carrier[:], 0.0)
                for j in range(TB):
                    dve.bn_aggr(mv[:, j, :], stats[:, j, :]).then_inc(stats_step, 1)

            def prep_normalise(b):
                dve.wait_ge(rstd_done, b + 1)
                dve.wait_ge(stats_step, STATS * (b + 1))
                if not first(b):
                    dve.wait_ge(xn_turned, b)
                for j in range(TB):
                    dve.tensor_scalar(xn[:, j, :], x[:, ds(TB * b + j, 1), :].squeeze(1), mv[:, j, 0:1],
                                      rstd[:, j:j + 1], ALU.subtract, ALU.mult).then_inc(xn_done, 1)

            def split_x(b):
                dve.wait_ge(x_hi_done, b + 1)
                dve.tensor_tensor(x_lo[:], t_ps[:, 0:SEQ], x_hi[:].bitcast(F32), ALU.subtract).then_inc(x_lo_done, 1)

            def split_qk(b, par, g):
                dve.wait_ge(f_done, 2 * (QT * b + g + 1))
                for k in range(2):
                    part = qk[par][:, 2 * g + k, :]
                    low = const[:, C_QLOW + k:C_QLOW + k + 1]
                    last = dve.scalar_tensor_tensor(part, part.bitcast(F32), low, f[g % F_RING][:, k, :], ALU.mult, ALU.add)
                last.then_inc(qk_done, 1)

            def take_vg(b, par, j):
                dve.wait_ge(projected, ITEMS * b + QT + j + 1)
                if not first(b) and not (isinstance(b, int) and b < 2):
                    dve.wait_ge(mixed, PAIRS * (b - 1))
                    dve.wait_ge(r_gated, b - 1)
                flat = p_ps[:].rearrange("p a b -> p (a b)")
                pairs = "p (q i d) -> p q i d"
                dve.tensor_tensor(v[par][:, j, :, 0:3:2, :], flat[:, 0:VB].rearrange(pairs, q=PAIRS, i=2),
                                  bvg[:, 0:VB].rearrange(pairs, q=PAIRS, i=2), ALU.add)
                dve.tensor_tensor(gates[par][:, j, :], flat[:, VB:2 * VB], bvg[:, VB:2 * VB], ALU.add)\
                   .then_inc(vg_done, 1)

            def apply_mask(b, p):
                dve.wait_ge(scored, PAIRS * b + p + 1)
                if not first(b) or p >= M_RING:
                    dve.wait_ge(mixed, PAIRS * b + last_use(p, M_RING) + 1)
                    dve.wait_ge(abs_done, PAIRS * b + last_use(p, M_RING) + 1)
                dve.tensor_tensor(masked[p % M_RING][:], s_ps[:, p % S_RING, :, P:4 * P], mask[:, 2 * p:2 * p + 2, :],
                                  ALU.mult).then_inc(mask_done, 1)

            def norm_denominator(b):
                base = NORM * b
                dve.wait_ge(sums_turned, b + 1)
                if not first(b):
                    dve.wait_ge(norm_step, base)
                taken = t_ps[:, 0:SEQ].rearrange("p (j i k) -> p j i k", j=TB, k=32)[:, :, :, 0:HEADS // 4]
                dve.tensor_scalar(denom[:].rearrange("p (j k i) -> p j i k", j=TB, i=4), taken, DENOM_LO, DENOM_HI,
                                  ALU.max, ALU.min).then_inc(norm_step, 1)
                dve.wait_ge(norm_step, base + 1)
                dve.scalar_tensor_tensor(denom[:], denom[:], RMS_EPS, denom[:], ALU.mult, ALU.mult).then_inc(norm_step, 1)

            def norm_power(b):
                base = NORM * b
                dve.wait_ge(norm_step, base + 2)
                dve.wait_ge(square_done, b + 1)
                if not first(b):
                    dve.wait_ge(norm_applied, b)
                dve.tensor_reduce(ssum[:], square[:].rearrange("p (h d) -> p h d", d=VD), AX.X, ALU.add).then_inc(norm_step, 1)
                dve.wait_ge(norm_step, base + 3)
                dve.scalar_tensor_tensor(ssum[:], ssum[:], 1.0 / VD, denom[:], ALU.mult, ALU.add).then_inc(norm_step, 1)

            def norm_scale(b):
                dve.wait_ge(root_done, b + 1)
                dve.reciprocal(ssum[:], ssum[:]).then_inc(norm_step, 1)

            def norm_apply(b):
                wide = r_sb[:].rearrange("p (h d) -> p h d", d=VD)
                dve.wait_ge(r_gated, b + 1)
                dve.wait_ge(norm_step, NORM * (b + 1))
                dve.tensor_tensor(wide, wide, ssum[:].unsqueeze(2).to_broadcast([P, TB * HEADS, VD]), ALU.mult)\
                   .then_inc(norm_applied, 1)

            def update(b):
                dve.wait_ge(out_done, b + 1)
                dve.wait_ge(bias_added, b + 1)
                rows = x[:, ds(TB * b, TB), :].rearrange("p j c -> p (j c)")
                dve.tensor_tensor(rows, t_ps[:, 0:SEQ], rows, ALU.add).then_inc(x_updated, 1)

            def sequence(b, par, prep=True):
                for p in range(PAIRS):
                    apply_mask(b, p)
                    if p == 7 and prep and not is_second_last(b):
                        prep_normalise(b + 2)
                    if prep and p >= 6:
                        take_vg(b + 1, 1 - par, p - 6)
                    if prep:
                        if p == 0:
                            split_x(b + 1)
                        elif 2 <= p <= QT + 1:
                            split_qk(b + 1, 1 - par, p - 2)
                        if p == 6 and not is_second_last(b):
                            prep_stats(b + 2)
                    if not isinstance(b, int) or b > 1:
                        if p == 0:
                            norm_apply(b - 2)
                        if p == 3:
                            update(b - 2)
                    if not first(b):
                        if p == 6:
                            norm_denominator(b - 1)
                            norm_power(b - 1)
                        if p == 7:
                            norm_scale(b - 1)

            def is_second_last(b):
                return isinstance(b, int) and b == seqs - 2

            dve.memset(half_neg[:], -0.5)
            dve.memset(eps[:], LN_EPS).then_inc(preset, 1)
            for i in range(2):
                dve.memset(v[i][:, :, :, 1, :], 0.0)
            dve.memset(pick[:], 0.0).then_inc(preset, 1)
            dve.wait_ge(preset, 2)
            dve.memset(pick[:, HEADS // 4 - 1:HEADS // 4], 1.0).then_inc(preset, 1)
            prep_stats(0)
            prep_normalise(0)
            for k, (lo, src, hi) in enumerate(((wqk_lo, w_qk, wqk_hi), (wvg_lo, w_vg, wvg_hi))):
                dve.wait_ge(split_hi, k + 1)
                dve.tensor_tensor(lo[:], src, hi[:].bitcast(F32), ALU.subtract).then_inc(split_lo, 1)
            dve.wait_ge(split_lo, 2)
            split_x(0)
            for g in range(QT):
                split_qk(0, 0, g)
            for j in range(TB):
                take_vg(0, 0, j)
            prep_stats(1)
            prep_normalise(1)
            dve.wait_ge(loaded_mask, 16)
            sequence(0, 0)
            sequence(1, 1)
            with dve.Fori(1, seqs // 2 - 1) as two:
                sequence(2 * two, 0)
                sequence(2 * two + 1, 1)
            sequence(seqs - 2, 0)
            sequence(seqs - 1, 1, prep=False)
            norm_apply(seqs - 2)
            update(seqs - 2)
            norm_denominator(seqs - 1)
            norm_power(seqs - 1)
            norm_scale(seqs - 1)
            norm_apply(seqs - 1)
            update(seqs - 1)

        @block.gpsimd
        def _(pool):
            def prep_rstd(b):
                pool.wait_ge(stats_step, STATS * (b + 1))
                if not first(b):
                    pool.wait_ge(xn_done, TB * b)
                pool.tensor_tensor(veps[:], mv[:, :, 1], eps[:], ALU.add).then_inc(var_eps, 1)
                pool.wait_ge(var_eps, b + 1)
                pool.tensor_tensor(rstd[:], veps[:], half_neg[:], ALU.pow).then_inc(rstd_done, 1)

            def add_bias(b):
                pool.wait_ge(xn_done, TB * (b + 1))
                rows = x[:, ds(TB * b, TB), :]
                pool.tensor_tensor(rows, rows, bo[:].unsqueeze(1).to_broadcast([P, TB, P]), ALU.add).then_inc(bias_added, 1)

            def apply_gates(b, par):
                pool.wait_ge(r_taken, b + 1)
                flat = r_sb[:].rearrange("p (j c) -> p j c", j=TB)
                pool.tensor_tensor(flat, flat, gates[par][:], ALU.mult).then_inc(r_gated, 1)

            def sequence(b, par, prep=True):
                if prep:
                    add_bias(b + 1)
                if not first(b):
                    apply_gates(b - 1, 1 - par)
                if prep and not (isinstance(b, int) and b == seqs - 2):
                    prep_rstd(b + 2)

            pool.wait_ge(preset, 3)
            prep_rstd(0)
            pool.wait_ge(loaded, 96)
            add_bias(0)
            prep_rstd(1)
            sequence(0, 0)
            sequence(1, 1)
            with pool.Fori(1, seqs // 2 - 1) as two:
                sequence(2 * two, 0)
                sequence(2 * two + 1, 1)
            sequence(seqs - 2, 0)
            sequence(seqs - 1, 1, prep=False)
            apply_gates(seqs - 1, 1)


def build(nc, x, const, mask, w_qk, b_qk, w_vg, b_vg, w_o, b_o, wfc_s, wproj_s, wr, wfc, wproj, b_up, b_down,
          gate_scratch, out):
    tokens = x.shape[0]
    ctx = ExitStack()
    with ctx:
        def sb(n, shape, dt=F32):
            return ctx.enter_context(nc.sbuf_tensor(n, shape, dt))

        m = {
            "tokens": tokens,
            "x": sb("x", [P, tokens // P, P]),
            "w_hi": sb("w_hi", [P, EX, 2 * HID], F32R),
            "w_lo": sb("w_lo", [P, EX, 2 * HID], F32R),
            "const": sb("const", [P, C_END]),
            "x_dram": x.rearrange("(n p) c -> p n c", p=P),
            "out_dram": out.rearrange("(n p) c -> p n c", p=P),
            "const_dram": const, "wr_dram": wr, "b_up_dram": b_up, "b_down_dram": b_down,
            "w_dram": [(wfc_s, wproj_s.rearrange("(c p) n -> p c n", p=P))]
                      + [(wfc[e], wproj[e].rearrange("(c p) n -> p c n", p=P)) for e in range(NE)],
            "gate_dram": gate_scratch,
            "mask_dram": mask, "w_qk_dram": w_qk, "b_qk_dram": b_qk, "w_vg_dram": w_vg, "b_vg_dram": b_vg,
            "w_o_dram": w_o.rearrange("(k p) n -> p k n", p=P), "b_o_dram": b_o,
        }
        ffn_phase(nc, m, "ffn1", load=True, store=False)
        retention_phase(nc, m)
        ffn_phase(nc, m, "ffn2", load=False, store=True)


def decay_mask():
    gamma = np.log(1.0 - 2.0 ** (-5.0 - np.arange(HEADS)))
    at = np.arange(SEQ)
    diff = at[:, None] - at[None, :]
    decay = np.where(diff >= 0, np.exp(gamma[:, None, None] * np.maximum(diff, 0)), 0.0)
    full = (decay / np.sqrt(decay.sum(-1, keepdims=True))).transpose(2, 0, 1)
    blocks = (full[P:, :, P:], full[:P, :, :P], full[:P, :, P:])
    return np.ascontiguousarray(np.concatenate(blocks, axis=2)).astype(np.float32)


def constants():
    c = np.zeros((P, C_END), np.float32)
    c[:, C_ID:C_ID + P] = np.eye(P)
    c[:, C_IOTA:C_IOTA + NE] = np.arange(NE)
    copy = np.arange(P) // KD % 4
    c[:, C_QLOW] = np.where(copy >= 2, -1.0, 0.0)
    c[:, C_KLOW] = np.where(copy % 2 == 1, -1.0, 0.0)
    return c


def kernel(L0_attn_x, L0_attn_W_qk, L0_attn_b_qk, L0_attn_W_v, L0_attn_b_v, L0_attn_W_g, L0_attn_b_g,
           L0_attn_W_o, L0_attn_b_o, L0_ffn_Wfc_s, L0_ffn_bfc_s, L0_ffn_Wproj_s, L0_ffn_bproj_s, L0_ffn_Wr,
           L0_ffn_Wfc, L0_ffn_bfc, L0_ffn_Wproj, L0_ffn_bproj):
    import concourse.bacc as bacc
    from concourse.bass_utils import run_bass_kernel_spmd

    g, kind, j, copy, d = np.ix_(range(QT), range(2), range(4), range(4), range(KD))
    spread = (kind * P + (4 * g + j) * KD + d + 0 * copy).reshape(-1)
    shape = np.shape(L0_attn_x)
    arrays = {
        "x": np.reshape(L0_attn_x, (-1, P)),
        "const": constants(),
        "mask": decay_mask(),
        "w_qk": np.asarray(L0_attn_W_qk)[:, spread],
        "b_qk": np.asarray(L0_attn_b_qk)[spread].reshape(2 * QT, P).T,
        "w_vg": np.concatenate([L0_attn_W_v, L0_attn_W_g], axis=1),
        "b_vg": np.concatenate([L0_attn_b_v, L0_attn_b_g]),
        "w_o": L0_attn_W_o,
        "b_o": L0_attn_b_o,
        "wfc_s": L0_ffn_Wfc_s,
        "wproj_s": L0_ffn_Wproj_s,
        "wr": L0_ffn_Wr,
        "wfc": L0_ffn_Wfc,
        "wproj": L0_ffn_Wproj,
        "b_up": np.concatenate([np.reshape(L0_ffn_bfc_s, (1, HID)), L0_ffn_bfc]).reshape(EX * CH, P).T,
        "b_down": np.concatenate([L0_ffn_bproj, np.reshape(L0_ffn_bproj_s, (1, P))]),
    }
    nc = bacc.Bacc("TRN2", target_bir_lowering=False, num_devices=1)
    feeds, args = {}, []
    for name, a in arrays.items():
        a = np.ascontiguousarray(a)
        feeds[f"in_{name}"] = a
        args.append(nc.dram_tensor(f"in_{name}", a.shape, mybir.dt.from_np(a.dtype), kind="ExternalInput").ap())
    args.append(nc.dram_tensor("gate_scratch", (NE, TOK), F32).ap())
    args.append(nc.dram_tensor("out", feeds["in_x"].shape, F32, kind="ExternalOutput").ap())
    build(nc, *args)
    result = run_bass_kernel_spmd(nc, [feeds], core_ids=[0])
    return np.reshape(result.results[0]["out"], shape)
```

```python
from contextlib import ExitStack

import numpy as np
import concourse.bass as bass
from concourse import mybir

F32 = mybir.dt.float32
F32R = mybir.dt.float32r
U32 = mybir.dt.uint32
I32 = mybir.dt.int32
ALU = mybir.AluOpType
ACT = mybir.ActivationFunctionType
AX = mybir.AxisListType
ds = bass.ds

P = 128
SEQ = 256
HEADS, KD, VD = 16, 8, 16
VB = HEADS * VD
HID = 512
NE = 8
EX = NE + 1
JOB = 512
SUB = JOB // P
CH = HID // P
TOKENS = 32 * SEQ
MOST = TOKENS // JOB
HALF_JOBS = MOST + NE - 1
JOBS = 2 * HALF_JOBS
LN_EPS = 1e-5
RMS_EPS = float(np.finfo(np.float32).eps)
DENOM_LO, DENOM_HI = 1.0, 50000.0
UP_RING, G_RING = 3, 16
PAIRS = HEADS // 2
QT = 4
S_RING, M_RING, A_RING, F_RING = 2, 3, 3, 2
ROUTE = 15
CAUSAL = 3 * P
C_ID, C_BEFORE, C_IOTA = 0, P, 2 * P
C_QLOW, C_KLOW = C_IOTA + NE, C_IOTA + NE + 1
C_LOWER = C_KLOW + 1
C_FULL = C_LOWER + NE * NE
C_JOB = C_FULL + MOST
C_SAME = C_JOB + HALF_JOBS
C_END = C_SAME + 2 * P


def ffn_phase(nc, m, name, load, store):
    tiles = m["tokens"] // JOB
    blocks = m["tokens"] // P
    all_jobs = tiles + JOBS
    middle = tiles + HALF_JOBS
    ctx = ExitStack()
    with ctx:
        def sb(n, shape, dt=F32):
            return ctx.enter_context(nc.sbuf_tensor(f"{name}_{n}", shape, dt))

        def pb(n, cols=512):
            return ctx.enter_context(nc.psum_tensor(f"{name}_{n}", [P, cols], F32))

        def sem(n):
            return ctx.enter_context(nc.semaphore(f"{name}_{n}"))

        x, w_hi, w_lo, const = m["x"], m["w_hi"], m["w_lo"], m["const"]
        ident, before = const[:, C_ID:C_ID + P], const[:, C_BEFORE:C_BEFORE + P]
        same_half = const[:, C_SAME:C_SAME + P]
        wr, biases = sb("wr", [P, NE]), sb("biases", [P, EX, CH + 1])
        xn = sb("xn", [P, blocks, P])
        xf = [sb(f"xf{i}", [P, JOB]) for i in range(2)]
        stats = [sb(f"stats{i}", [P, SUB, 6]) for i in range(2)]
        mv = [sb(f"mv{i}", [P, SUB, 2]) for i in range(2)]
        veps, rstd = sb("veps", [P, SUB]), [sb(f"rstd{i}", [P, SUB]) for i in range(2)]
        eps, half_neg = sb("eps", [P, SUB]), sb("half_neg", [P, SUB])
        carrier = sb("carrier", [P, 1])
        euler, gap, egap, egap1 = (sb(n, [P, blocks]) for n in ("euler", "gap", "egap", "egap1"))
        gate = sb("gate", [P, 2, blocks])
        best = [sb(f"best{i}", [P, blocks]) for i in range(2)]
        number, total = sb("number", [P, blocks]), sb("total", [P, 2 * NE])
        logits = sb("logits", [P, blocks, NE])
        chosen = sb("chosen", [P, NE, 2 * blocks])
        counts = sb("counts", [P, NE])
        ones = sb("ones", [P, P])
        passed = sb("passed", [P, 2 * NE, MOST])
        jobs_of, start, end, start_slot = (sb(n, [P, 2 * NE]) for n in ("jobs_of", "start", "end", "start_slot"))
        pairs = sb("pairs", [P, 2, NE, NE])
        ended, expert = sb("ended", [P, 2, HALF_JOBS, NE]), sb("expert", [P, JOBS])
        table = sb("table", [P, JOBS], I32)
        slot_f = sb("slot_f", [P, 2 * blocks])
        slot = sb("slot", [P, 2 * blocks], U32)
        xj = xf[1][:].rearrange("p (j c) -> p j c", j=SUB)
        x_hi, x_lo = sb("x_hi", [P, JOB], F32R), sb("x_lo", [P, JOB], F32R)
        h = [sb(f"h{i}", [P, 2 * JOB]) for i in range(4)]
        h_hi = [sb(f"h_hi{i}", [P, 2 * JOB], F32R) for i in range(2)]
        h_lo = [sb(f"h_lo{i}", [P, 2 * JOB], F32R) for i in range(2)]
        w_up = [sb(f"w_up{i}", [P, 2, HID], F32R) for i in range(2)]
        w_down = sb("w_down", [P, 2, HID], F32R)
        equal, key = (h[1][:, i * JOB:(i + 1) * JOB].rearrange("p (n e) -> p n e", e=NE) for i in range(2))
        counts_wide, slot_part = (h[i][:].rearrange("p (e c) -> p e c", e=NE) for i in range(2))
        bias_up, bias_down = [sb(f"bias_up{i}", [P, CH]) for i in range(2)], sb("bias_down", [P, 1])
        y_sb, y_rows = xf[0], sb("y_rows", [P, SUB, P])
        gathered_at = [h[i // 8][:, (i % 8) * P:(i % 8 + 1) * P] for i in range(G_RING)]
        stage = [h[i][:] for i in range(4)]

        up_ps = [pb(f"up{i}") for i in range(UP_RING)]
        y_ps, t_ps, b_ps = pb("y"), pb("t"), pb("b")
        r_ps = pb("r", 1024)

        loaded_x = [sem(f"loaded_x{i}") for i in range(3)]
        loaded_small, loaded_const = sem("loaded_small"), sem("loaded_const")
        loaded_w = [sem(f"loaded_w{e}") for e in range(EX)] if load else None
        w_hi_done, w_lo_done = sem("w_hi_done"), sem("w_lo_done")
        cleared, stored, preset = sem("cleared"), sem("stored"), sem("preset")
        stats_step, var_eps, rstd_done, xn_done = sem("stats_step"), sem("var_eps"), sem("rstd_done"), sem("xn_done")
        xn_turned, xf_done, logits_done = sem("xn_turned"), sem("xf_done"), sem("logits_done")
        route, gap_done, egap_done, gate_step = sem("route"), sem("gap_done"), sem("egap_done"), sem("gate_step")
        counted, placed, totalled = sem("counted"), sem("placed"), sem("totalled")
        table_done, slots_done = sem("table_done"), sem("slots_done")
        x_loaded, x_turned, x_hi_done, x_lo_done = sem("x_loaded"), sem("x_turned"), sem("x_hi_done"), sem("x_lo_done")
        up_ready, down_ready = sem("up_ready"), sem("down_ready")
        up_done, gelu_done, hi_done, lo_done = sem("up_done"), sem("gelu_done"), sem("hi_done"), sem("lo_done")
        down_half, y_taken, y_turned = sem("down_half"), sem("y_taken"), sem("y_turned")
        rows_done, y_stored, x_updated = sem("rows_done"), sem("y_stored"), sem("x_updated")
        scattered, gathered = m["scattered"], m["gathered"]
        gathered_half = m["gathered_half"]
        rounds = blocks // G_RING
        before_now, rounds_before = (0, 0) if load else (blocks, rounds)
        combined = sem("combined")
        STATS = 2 * SUB
        block = ctx.enter_context(nc.Block())

        def first(t):
            return isinstance(t, int) and t == 0

        def rows_of(dram, t, half):
            return dram[half][:, ds(SUB * t - SUB * (tiles + half * HALF_JOBS), SUB), :]

        @block.sync
        def _(sp):
            if load:
                sp.dma_start(x[:, 0:2 * SUB, :], m["x_dram"][:, 0:2 * SUB, :]).then_inc(loaded_x[0], 16)
                sp.dma_start(const[:], m["const_dram"]).then_inc(loaded_const, 16)
            for dst, src in ((wr[:], m["wr_dram"]), (biases[:], m["bias_dram"])):
                sp.dma_start(dst, src).then_inc(loaded_small, 16)
            if load:
                sp.dma_start(x[:, 2 * SUB:6 * SUB, :], m["x_dram"][:, 2 * SUB:6 * SUB, :]).then_inc(loaded_x[1], 16)
                for e in range(EX):
                    if e >= 4:
                        sp.wait_ge(w_lo_done, e - 3)
                    up, down = m["w_dram"][e]
                    sp.dma_start(stage[e % 4][:, 0:HID], up).then_inc(loaded_w[e], 16)
                    sp.dma_start(stage[e % 4][:, HID:].rearrange("p (c n) -> p c n", c=CH), down)\
                      .then_inc(loaded_w[e], 16)
                    if e == 1:
                        sp.dma_start(x[:, 6 * SUB:, :], m["x_dram"][:, 6 * SUB:, :]).then_inc(loaded_x[2], 16)
                sp.wait_ge(preset, 2)
                for t in range(JOBS):
                    at = SUB * (t % HALF_JOBS)
                    sp.dma_start(m["x_slots"][t // HALF_JOBS][:, at:at + SUB, :], y_rows[:]).then_inc(cleared, 16)

            def load_job(t, half=None):
                if not first(t):
                    sp.wait_ge(x_turned, t)
                src = rows_of(m["x_slots"], t, half) if half is not None else xn[:, ds(SUB * t, SUB), :]
                sp.dma_start(xj, src).then_inc(x_loaded, 16)

            sp.wait_ge(xn_done, blocks)
            sp.wait_ge(logits_done, tiles)
            load_job(0)
            with sp.Fori(1, tiles) as t:
                load_job(t)
            sp.wait_ge(scattered[0], 16 * (before_now + blocks))
            with sp.Fori(tiles, middle) as t:
                load_job(t, 0)
            sp.wait_ge(scattered[1], 16 * (before_now + blocks))
            with sp.Fori(middle, all_jobs) as t:
                load_job(t, 1)
            sp.wait_ge(y_stored, 16 * JOBS)
            if store:
                for t in range(tiles):
                    sp.wait_ge(combined, 2 * SUB * (t + 1))
                    sp.dma_start(m["out_dram"][:, SUB * t:SUB * (t + 1), :], x[:, SUB * t:SUB * (t + 1), :])\
                      .then_inc(stored, 16)
                sp.wait_ge(stored, 16 * tiles)

        @block.tensor
        def _(pe):
            def route_turn(t):
                pe.wait_ge(xn_done, SUB * (t + 1))
                if t >= 2:
                    pe.wait_ge(xf_done, t - 1)
                bank = (t_ps, b_ps)[t % 2]
                for j in range(SUB):
                    last = pe.transpose(bank[:, j * P:(j + 1) * P], xn[:, SUB * t + j, :], ident)
                last.then_inc(xn_turned, 1)

            def route_logits(t):
                pe.wait_ge(xf_done, t + 1)
                for j in range(SUB):
                    last = pe.matmul(r_ps[:, (SUB * t + j) * NE:(SUB * t + j + 1) * NE], xf[t % 2][:, j * P:(j + 1) * P], wr[:],
                                     start=True, stop=True)
                last.then_inc(logits_done, 1)

            def place():
                pe.wait_ge(route, ROUTE)
                for e in range(NE):
                    last = pe.matmul(t_ps[:, e:e + 1], chosen[:, e, :], ones[:, 0:1], start=True, stop=True)
                last.then_inc(counted, 1)
                pe.wait_ge(route, ROUTE + 2)
                second = const[:, C_SAME + P:C_END]
                pe.matmul(b_ps[:, 0:NE], ones[:], counts[:], start=True, stop=True)
                pe.matmul(b_ps[:, NE:2 * NE], second, counts[:], start=True, stop=True).then_inc(totalled, 1)
                for e in range(NE):
                    out = r_ps[:, e * P:(e + 1) * P]
                    pe.matmul(out, before, chosen[:, e, :], start=True, stop=False)
                    last = pe.matmul(out, counts_wide[:, e, :], same_half, start=False, stop=True)
                last.then_inc(placed, 1)

            def turn(t):
                pe.wait_ge(x_loaded, 16 * (t + 1))
                for j in range(SUB):
                    last = pe.transpose(t_ps[:, j * P:(j + 1) * P], xj[:, j, :], ident)
                last.then_inc(x_turned, 1)

            def up(t, par, routed):
                pe.wait_ge(x_lo_done, t + 1)
                if routed:
                    pe.wait_ge(up_ready, t - tiles + 1)
                parts = (w_up[par][:, 0, :], w_up[par][:, 1, :]) if routed else (w_hi[:, 0, 0:HID], w_lo[:, 0, 0:HID])
                for c in range(CH):
                    q = CH * t + c
                    if c == 0 and not first(t) or c >= UP_RING:
                        pe.wait_ge(gelu_done, q if c == 0 else q - UP_RING + 1)
                    bank = up_ps[c % UP_RING]
                    hi, lo = (part[:, c * P:(c + 1) * P] for part in parts)
                    pe.matmul(bank[:], hi, x_hi[:], start=True, stop=False)
                    pe.matmul(bank[:], hi, x_lo[:], start=False, stop=False)
                    pe.matmul(bank[:], lo, x_hi[:], start=False, stop=True).then_inc(up_done, 1)

            def down(t, routed):
                if not first(t):
                    pe.wait_ge(y_taken, t)
                if routed:
                    pe.wait_ge(down_ready, t - tiles + 1)
                parts = (w_down[:, 0, :], w_down[:, 1, :]) if routed else (w_hi[:, 0, HID:], w_lo[:, 0, HID:])
                for c in range(CH):
                    if c % 2 == 0:
                        pe.wait_ge(lo_done, 2 * t + c // 2 + 1)
                    cols = slice((c % 2) * JOB, (c % 2 + 1) * JOB)
                    hi, lo = (part[:, c * P:(c + 1) * P] for part in parts)
                    a_hi, a_lo = h_hi[c // 2][:, cols], h_lo[c // 2][:, cols]
                    pe.matmul(y_ps[:], hi, a_hi, start=(c == 0), stop=False)
                    pe.matmul(y_ps[:], hi, a_lo, start=False, stop=False)
                    last = pe.matmul(y_ps[:], lo, a_hi, start=False, stop=(c == CH - 1))
                    if c % 2:
                        last.then_inc(down_half, 1)

            def back(t, routed):
                pe.wait_ge(y_taken, t + 1)
                if not routed:
                    if not first(t):
                        pe.wait_ge(x_updated, t)
                elif isinstance(t, int) and t == tiles:
                    pe.wait_ge(x_updated, tiles)
                else:
                    pe.wait_ge(rows_done, t - tiles)
                for j in range(SUB):
                    last = pe.transpose(b_ps[:, j * P:(j + 1) * P], y_sb[:, j * P:(j + 1) * P], ident)
                last.then_inc(y_turned, 1)

            def job(t, par, routed, before=None, two_before=None, more=True):
                up(t, par, routed)
                if more:
                    turn(t + 1)
                if two_before is not None:
                    back(t - 2, two_before)
                if before is not None:
                    down(t - 1, before)

            pe.wait_ge(preset, 1)
            pe.wait_ge(loaded_small, 32)
            if load:
                pe.wait_ge(loaded_const, 16)
            for t in range(tiles):
                route_turn(t)
                if t:
                    route_logits(t - 1)
            route_logits(tiles - 1)
            place()
            turn(0)
            if load:
                pe.wait_ge(w_lo_done, EX)
            job(0, 0, False)
            job(1, 1, False, False)
            with pe.Fori(1, tiles // 2) as two:
                job(2 * two, 0, False, False, False)
                job(2 * two + 1, 1, False, False, False)
            job(tiles, 0, True, False, False)
            job(tiles + 1, 1, True, True, False)
            job(tiles + 2, 0, True, True, True)
            job(tiles + 3, 1, True, True, True)
            with pe.Fori(tiles // 2 + 2, all_jobs // 2 - 1) as two:
                job(2 * two, 0, True, True, True)
                job(2 * two + 1, 1, True, True, True)
            job(all_jobs - 2, 0, True, True, True)
            job(all_jobs - 1, 1, True, True, True, more=False)
            back(all_jobs - 2, True)
            down(all_jobs - 1, True)
            back(all_jobs - 1, True)

        @block.scalar
        def _(act):
            def route_take(t):
                act.wait_ge(xn_turned, t + 1)
                if t >= 2:
                    act.wait_ge(logits_done, t - 1)
                act.activation(xf[t % 2][:], (t_ps, b_ps)[t % 2][:], ACT.Copy).then_inc(xf_done, 1)

            def split_weights(e):
                act.wait_ge(loaded_w[e], 32)
                act.activation(w_hi[:, e, :], stage[e % 4], ACT.Copy).then_inc(w_hi_done, 1)

            def take_x(t):
                act.wait_ge(x_turned, t + 1)
                if not first(t):
                    act.wait_ge(up_done, CH * t)
                act.activation(x_hi[:], t_ps[:], ACT.Copy).then_inc(x_hi_done, 1)

            def place_down(t):
                e = act.value_load(table[0:1, ds(t - tiles, 1)], min_val=1, max_val=NE)
                for i, part in enumerate((w_hi, w_lo)):
                    act.activation(w_down[:, i, :], part[:, ds(e, 1), HID:].squeeze(1), ACT.Copy)
                act.activation(bias_down[:], biases[:, ds(e, 1), CH:CH + 1].squeeze(1), ACT.Copy).then_inc(down_ready, 1)

            def hidden(t, par, routed, down_before):
                if routed:
                    act.wait_ge(up_ready, t - tiles + 1)
                bias = bias_up[par][:] if routed else biases[:, 0, 0:CH]
                for c in range(CH):
                    if c == 0 and down_before:
                        act.wait_ge(y_taken, t - 1)
                    if c % 2 == 0 and (not isinstance(t, int) or t >= 2):
                        act.wait_ge(lo_done, 2 * t - 3 + c // 2)
                    act.wait_ge(up_done, CH * t + c + 1)
                    act.activation(h[2 * par + c // 2][:, (c % 2) * JOB:(c % 2 + 1) * JOB], up_ps[c % UP_RING][:],
                                   ACT.Gelu_apprx_tanh, bias=bias[:, c:c + 1]).then_inc(gelu_done, 1)
                    if c == 1 and down_before:
                        place_down(t - 1)

            def take_y(t, routed):
                act.wait_ge(down_half, 2 * t + 2)
                if routed:
                    act.wait_ge(down_ready, t - tiles + 1)
                if not first(t):
                    act.wait_ge(y_turned, t)
                act.activation(y_sb[:], y_ps[:], ACT.Identity,
                               bias=bias_down[:] if routed else biases[:, 0, CH:CH + 1]).then_inc(y_taken, 1)

            def take_rows(t, half):
                act.wait_ge(y_turned, t + 1)
                if not isinstance(t, int) or t > tiles:
                    act.wait_ge(y_stored, 16 * (t - tiles))
                act.activation(y_rows[:].rearrange("p j c -> p (j c)"), b_ps[:], ACT.Copy).then_inc(rows_done, 1)
                act.wait_ge(rows_done, t - tiles + 1)
                act.dma_start(rows_of(m["y_slots"], t, half), y_rows[:]).then_inc(y_stored, 16)

            def job(t, par, routed, before=False, two_before=None, turn_next=True, half=0):
                if two_before is not None:
                    take_y(t - 2, two_before)
                hidden(t, par, routed, before)
                if turn_next:
                    take_x(t + 1)
                if two_before:
                    take_rows(t - 2, half)

            act.wait_ge(loaded_small, 32)
            for t in range(tiles):
                route_take(t)
                if load and t < EX:
                    split_weights(t)
            take_x(0)
            job(0, 0, False)
            job(1, 1, False)
            with act.Fori(1, tiles // 2) as two:
                job(2 * two, 0, False, False, False)
                job(2 * two + 1, 1, False, False, False)
            act.wait_ge(table_done, 1)
            job(tiles, 0, True, False, False)
            job(tiles + 1, 1, True, True, False)
            if load:
                act.wait_ge(cleared, 16 * JOBS)
            job(tiles + 2, 0, True, True, True)
            job(tiles + 3, 1, True, True, True)
            with act.Fori(tiles // 2 + 2, middle // 2 + 1) as two:
                job(2 * two, 0, True, True, True)
                job(2 * two + 1, 1, True, True, True)
            job(middle + 1, 0, True, True, True)
            job(middle + 2, 1, True, True, True, half=1)
            with act.Fori(middle // 2 + 2, all_jobs // 2 - 1) as two:
                job(2 * two, 0, True, True, True, half=1)
                job(2 * two + 1, 1, True, True, True, half=1)
            job(all_jobs - 2, 0, True, True, True, half=1)
            job(all_jobs - 1, 1, True, True, True, turn_next=False, half=1)
            take_y(all_jobs - 2, True)
            act.wait_ge(y_taken, all_jobs - 1)
            place_down(all_jobs - 1)
            take_rows(all_jobs - 2, 1)
            take_y(all_jobs - 1, True)
            take_rows(all_jobs - 1, 1)

        @block.vector
        def _(dve):
            def route_stats(t):
                if load:
                    dve.wait_ge(loaded_x[0 if t < 2 else 1 if t < 6 else 2], 16)
                if t >= 2:
                    dve.wait_ge(rstd_done, t - 1)
                for j in range(SUB):
                    dve.bn_stats(stats[t % 2][:, j, :], x[:, SUB * t + j, :]).then_inc(stats_step, 1)
                dve.wait_ge(stats_step, STATS * t + SUB)
                for j in range(SUB):
                    dve.bn_aggr(mv[t % 2][:, j, :], stats[t % 2][:, j, :]).then_inc(stats_step, 1)

            def route_normalise(t):
                dve.wait_ge(rstd_done, t + 1)
                for j in range(SUB):
                    dve.tensor_scalar(xn[:, SUB * t + j, :], x[:, SUB * t + j, :], mv[t % 2][:, j, 0:1],
                                      rstd[t % 2][:, j:j + 1], ALU.subtract, ALU.mult).then_inc(xn_done, 1)

            def split_weights(e):
                dve.wait_ge(w_hi_done, e + 1)
                dve.tensor_tensor(w_lo[:, e, :], stage[e % 4], w_hi[:, e, :].bitcast(F32), ALU.subtract)\
                   .then_inc(w_lo_done, 1)

            def choose():
                wide = [P, blocks, NE]
                iota = const[:, C_IOTA:C_IOTA + NE].unsqueeze(1).to_broadcast(wide)
                dve.wait_ge(logits_done, tiles)
                dve.tensor_copy(logits[:].rearrange("p n e -> p (n e)"), r_ps[:, 0:blocks * NE]).then_inc(route, 1)
                for k in range(2):
                    base = 1 + 8 * k
                    one_hot = chosen[:].rearrange("p e (h k n) -> p k h n e", h=2, k=2)[:, k]
                    dve.wait_ge(route, base)
                    dve.tensor_reduce(best[k][:], logits[:], AX.X, ALU.max).then_inc(route, 1)
                    dve.wait_ge(route, base + 1)
                    dve.tensor_tensor(equal, logits[:], best[k][:].unsqueeze(2).to_broadcast(wide), ALU.is_equal)\
                       .then_inc(route, 1)
                    dve.wait_ge(route, base + 2)
                    dve.tensor_tensor(key, equal, iota, ALU.mult).then_inc(route, 1)
                    dve.wait_ge(route, base + 3)
                    dve.tensor_reduce(number[:], key, AX.X, ALU.min).then_inc(route, 1)
                    dve.wait_ge(route, base + 4)
                    for half in range(2):
                        rows = slice(half * blocks // 2, (half + 1) * blocks // 2)
                        dve.tensor_tensor(one_hot[:, half], number[:, rows].unsqueeze(2).to_broadcast([P, blocks // 2, NE]),
                                          iota[:, rows], ALU.is_equal).then_inc(route, 1)
                    if k == 0:
                        dve.wait_ge(route, base + 6)
                        for half in range(2):
                            rows = slice(half * blocks // 2, (half + 1) * blocks // 2)
                            dve.scalar_tensor_tensor(logits[:, rows], one_hot[:, half], -1e30, logits[:, rows],
                                                     ALU.mult, ALU.add).then_inc(route, 1)
                dve.tensor_tensor(gap[:], best[1][:], best[0][:], ALU.subtract).then_inc(gap_done, 1)

            def place():
                dve.wait_ge(counted, 1)
                dve.tensor_copy(counts[:], t_ps[:, 0:NE]).then_inc(route, 1)
                dve.tensor_copy(counts_wide, t_ps[:, 0:NE].unsqueeze(2).to_broadcast([P, NE, P])).then_inc(route, 1)
                dve.wait_ge(totalled, 1)
                halves = "p (h e) -> p h e"
                base = ROUTE + 2
                dve.tensor_copy(total[:], b_ps[:, 0:2 * NE]).then_inc(route, 1)
                dve.wait_ge(route, base + 1)
                dve.tensor_tensor(total[:, 0:NE], total[:, 0:NE], total[:, NE:], ALU.subtract).then_inc(route, 1)
                dve.wait_ge(route, base + 2)
                most = [P, 2 * NE, MOST]
                dve.tensor_tensor(passed[:], total[:].unsqueeze(2).to_broadcast(most),
                                  const[:, C_FULL:C_FULL + MOST].unsqueeze(1).to_broadcast(most), ALU.is_gt).then_inc(route, 1)
                dve.wait_ge(route, base + 3)
                dve.tensor_reduce(jobs_of[:], passed[:], AX.X, ALU.add).then_inc(route, 1)
                dve.wait_ge(route, base + 4)
                lower = const[:, C_LOWER:C_LOWER + NE * NE].rearrange("p (a b) -> p a b", a=NE)
                for half in range(2):
                    dve.tensor_tensor(pairs[:, half], jobs_of[:, half * NE:(half + 1) * NE].unsqueeze(1)
                                      .to_broadcast([P, NE, NE]), lower, ALU.mult).then_inc(route, 1)
                dve.wait_ge(route, base + 6)
                dve.tensor_reduce(start[:].rearrange(halves, h=2), pairs[:], AX.X, ALU.add).then_inc(route, 1)
                dve.wait_ge(route, base + 7)
                dve.tensor_tensor(end[:], start[:], jobs_of[:], ALU.add).then_inc(route, 1)
                dve.tensor_scalar(start_slot[:], start[:], float(JOB), None, ALU.mult).then_inc(route, 1)
                dve.wait_ge(route, base + 9)
                jobs = [P, HALF_JOBS, NE]
                for half in range(2):
                    dve.tensor_tensor(ended[:, half], end[:, half * NE:(half + 1) * NE].unsqueeze(1).to_broadcast(jobs),
                                      const[:, C_JOB:C_JOB + HALF_JOBS].unsqueeze(2).to_broadcast(jobs), ALU.is_le)\
                       .then_inc(route, 1)
                dve.wait_ge(route, base + 11)
                dve.tensor_reduce(expert[:].rearrange("p (h j) -> p h j", h=2), ended[:], AX.X, ALU.add).then_inc(route, 1)
                dve.wait_ge(route, base + 12)
                dve.tensor_scalar(expert[:], expert[:], float(NE - 1), 1.0, ALU.min, ALU.add).then_inc(route, 1)
                dve.wait_ge(route, base + 13)
                dve.tensor_copy(table[:], expert[:]).then_inc(table_done, 1)
                dve.wait_ge(placed, 1)
                wide = [P, NE, blocks]
                for half in range(2):
                    cols = slice(half * blocks, (half + 1) * blocks)
                    dve.tensor_tensor(slot_part[:, :, cols], r_ps[:].rearrange("p (e c) -> p e c", e=NE)[:, :, cols],
                                      start_slot[:, half * NE:(half + 1) * NE].unsqueeze(2).to_broadcast(wide), ALU.add)\
                       .then_inc(route, 1)
                dve.wait_ge(route, base + 15)
                dve.tensor_tensor(slot_part, slot_part, chosen[:], ALU.mult).then_inc(route, 1)
                dve.wait_ge(route, base + 16)
                dve.tensor_reduce(slot_f[:], slot_part.rearrange("p e c -> p c e"), AX.X, ALU.add).then_inc(route, 1)
                dve.wait_ge(route, base + 17)
                dve.tensor_copy(slot[:], slot_f[:]).then_inc(slots_done, 1)

            def split_x(t):
                dve.wait_ge(x_hi_done, t + 1)
                dve.tensor_tensor(x_lo[:], t_ps[:], x_hi[:].bitcast(F32), ALU.subtract).then_inc(x_lo_done, 1)

            def split_h(t, par, s):
                buf = h[2 * par + s]
                dve.wait_ge(gelu_done, CH * t + 2 * s + 2)
                if not first(t):
                    dve.wait_ge(down_half, 2 * t - 1 + s)
                dve.tensor_copy(h_hi[s][:], buf[:]).then_inc(hi_done, 1)
                dve.wait_ge(hi_done, 2 * t + s + 1)
                dve.tensor_tensor(h_lo[s][:], buf[:], h_hi[s][:].bitcast(F32), ALU.subtract).then_inc(lo_done, 1)

            def place_up(t, par):
                e = dve.value_load(table[0:1, ds(t - tiles, 1)], min_val=1, max_val=NE)
                dve.wait_ge(gelu_done, CH * (t - 1))
                dve.memset(carrier[:], 0.0)
                for i, part in enumerate((w_hi, w_lo)):
                    dve.tensor_copy(w_up[par][:, i, :], part[:, ds(e, 1), 0:HID].squeeze(1))
                dve.tensor_copy(bias_up[par][:], biases[:, ds(e, 1), 0:CH].squeeze(1)).then_inc(up_ready, 1)

            def update(t):
                dve.wait_ge(y_turned, t + 1)
                rows = x[:, ds(SUB * t, SUB), :].rearrange("p j c -> p (j c)")
                dve.scalar_tensor_tensor(rows, b_ps[:], 0.5, rows, ALU.mult, ALU.add).then_inc(x_updated, 1)

            def job(t, par, updates=True, turn_next=True, routed_next=True):
                if turn_next and routed_next:
                    place_up(t + 1, 1 - par)
                if turn_next:
                    split_x(t + 1)
                if updates:
                    update(t - 2)
                split_h(t, par, 0)
                split_h(t, par, 1)

            def combine(half, k):
                n, choice = half * blocks // 2 + k // 2, k % 2
                if half:
                    dve.wait_ge(gathered[k % G_RING], 16 * (rounds_before + k // G_RING + 1))
                if choice:
                    dve.wait_ge(combined, half * blocks + k)
                y = gathered_at[k % G_RING] if half else xn[:, k, :]
                dve.scalar_tensor_tensor(x[:, n, :], y, gate[:, choice, n:n + 1], x[:, n, :],
                                         ALU.mult, ALU.add).then_inc(combined, 1)

            dve.memset(half_neg[:], -0.5)
            dve.memset(eps[:], LN_EPS)
            dve.memset(euler[:], float(np.e))
            dve.memset(ones[:], 1.0).then_inc(preset, 1)
            dve.memset(y_rows[:], 0.0).then_inc(preset, 1)
            if load:
                dve.wait_ge(loaded_const, 16)
            dve.wait_ge(loaded_small, 32)
            dve.wait_ge(preset, 1)
            for t in range(tiles):
                route_stats(t)
                if t:
                    route_normalise(t - 1)
                if load and 3 <= t < 3 + EX:
                    split_weights(t - 3)
            route_normalise(tiles - 1)
            choose()
            place()
            split_x(0)
            job(0, 0, updates=False, routed_next=False)
            job(1, 1, updates=False, routed_next=False)
            with dve.Fori(1, tiles // 2 - 1) as two:
                job(2 * two, 0, routed_next=False)
                job(2 * two + 1, 1, routed_next=False)
            job(tiles - 2, 0, routed_next=False)
            dve.wait_ge(table_done, 1)
            for t in range(tiles - 1, tiles + 2):
                job(t, t % 2)
            with dve.Fori(tiles // 2 + 1, all_jobs // 2 - 1) as two:
                job(2 * two, 0, updates=False)
                job(2 * two + 1, 1, updates=False)
            job(all_jobs - 2, 0, updates=False)
            job(all_jobs - 1, 1, updates=False, turn_next=False)
            dve.wait_ge(egap_done, 1)
            dve.tensor_scalar(egap1[:], egap[:], 2.0, 2.0, ALU.mult, ALU.add).then_inc(gate_step, 1)
            dve.wait_ge(gate_step, 1)
            dve.reciprocal(gate[:, 0, :], egap1[:]).then_inc(gate_step, 1)
            dve.wait_ge(gate_step, 2)
            dve.tensor_tensor(gate[:, 1, :], gate[:, 0, :], egap[:], ALU.mult).then_inc(gate_step, 1)
            dve.wait_ge(gate_step, 3)
            dve.wait_ge(x_updated, tiles)
            dve.wait_ge(gathered_half, 16 * (before_now + blocks))
            for half in range(2):
                for k in range(blocks):
                    combine(half, k)

        @block.gpsimd
        def _(pool):
            pool.wait_ge(preset, 1)
            for t in range(tiles):
                pool.wait_ge(stats_step, STATS * (t + 1))
                if t:
                    pool.wait_ge(rstd_done, t)
                pool.tensor_tensor(veps[:], mv[t % 2][:, :, 1], eps[:], ALU.add).then_inc(var_eps, 1)
                pool.wait_ge(var_eps, t + 1)
                if t >= 2:
                    pool.wait_ge(xn_done, SUB * (t - 1))
                pool.tensor_tensor(rstd[t % 2][:], veps[:], half_neg[:], ALU.pow).then_inc(rstd_done, 1)
            pool.wait_ge(slots_done, 1)
            pool.wait_ge(xn_done, blocks)
            if load:
                pool.wait_ge(cleared, 16 * JOBS)
            def slots_of(half, k):
                col = half * blocks + (k % 2) * (blocks // 2) + k // 2
                return bass.IndirectOffsetOnAxis(ap=slot[:, col:col + 1], axis=0)

            for half in range(2):
                for k in range(blocks):
                    pool.indirect_dma_start(m["x_slot_rows"][half], slots_of(half, k), xn[:, half * blocks // 2 + k // 2, :], None)\
                        .then_inc(scattered[half], 16)
            pool.wait_ge(gap_done, 1)
            pool.tensor_tensor(egap[:], euler[:], gap[:], ALU.pow).then_inc(egap_done, 1)
            for half in range(2):
                pool.wait_ge(scattered[half], 16 * (before_now + blocks))
            pool.wait_ge(x_loaded, 16 * tiles)
            pool.wait_ge(y_stored, 16 * HALF_JOBS)
            for k in range(blocks):
                pool.indirect_dma_start(xn[:, k, :], None, m["y_slot_rows"][0], slots_of(0, k)).then_inc(gathered_half, 16)
            pool.wait_ge(lo_done, 2 * all_jobs)
            pool.wait_ge(y_stored, 16 * JOBS)
            for k in range(blocks):
                if k >= G_RING:
                    pool.wait_ge(combined, blocks + k - G_RING + 1)
                pool.indirect_dma_start(gathered_at[k % G_RING], None, m["y_slot_rows"][1], slots_of(1, k))\
                    .then_inc(gathered[k % G_RING], 16)


def retention_phase(nc, m):
    seqs = m["tokens"] // SEQ
    TB = SEQ // P
    ctx = ExitStack()
    with ctx:
        def sb(n, shape, dt=F32):
            return ctx.enter_context(nc.sbuf_tensor(f"ret_{n}", shape, dt))

        def pb(n, shape):
            return ctx.enter_context(nc.psum_tensor(f"ret_{n}", shape, F32))

        def sem(n):
            return ctx.enter_context(nc.semaphore(f"ret_{n}"))

        x, const = m["x"], m["const"]
        ident = const[:, C_ID:C_ID + P]
        mask = sb("mask", [P, HEADS, CAUSAL])
        wqk_hi = sb("wqk_hi", [P, 2 * QT * P], F32R)
        wqk_lo = sb("wqk_lo", [P, 2 * QT * P], F32R)
        wvg_hi = sb("wvg_hi", [P, 2 * VB], F32R)
        wvg_lo = sb("wvg_lo", [P, 2 * VB], F32R)
        wo = sb("wo", [P, VB // P, P])
        bqk = sb("bqk", [P, 2 * QT])
        bvg = sb("bvg", [P, 2 * VB])
        bo = sb("bo", [P, P])
        f = [sb(f"f{i}", [P, 2, SEQ]) for i in range(F_RING)]
        qk = [sb(f"qk{i}", [P, 2 * QT, SEQ], F32R) for i in range(2)]
        v = [sb(f"v{i}", [P, TB, PAIRS, 3, VD]) for i in range(2)]
        gates = [sb(f"gates{i}", [P, TB, VB]) for i in range(2)]
        masked = [sb(f"masked{i}", [P, 2, CAUSAL]) for i in range(M_RING)]
        absed = [sb(f"absed{i}", [P, 2, CAUSAL]) for i in range(A_RING)]
        pick = sb("pick", [P, 32 + HEADS // 4 - 1])
        sums = sb("sums", [P, SEQ])
        xn = sb("xn", [P, TB, P])
        x_hi = sb("x_hi", [P, SEQ], F32R)
        x_lo = sb("x_lo", [P, SEQ], F32R)
        stats = sb("stats", [P, TB, 6])
        mv = sb("mv", [P, TB, 2])
        veps = sb("veps", [P, TB])
        rstd = sb("rstd", [P, TB])
        eps = sb("eps", [P, TB])
        carrier = sb("carrier", [P, 1])
        half_neg = sb("half_neg", [P, TB])
        r_turned = sb("r_turned", [P, TB * VB])
        r_sb = sb("r_sb", [P, TB * VB])
        square = sb("square", [P, TB * VB])
        denom = sb("denom", [P, TB * HEADS])
        ssum = sb("ssum", [P, TB * HEADS])
        gated_t = square

        w_qk = mask[:].rearrange("p h c -> p (h c)")[:, 0:2 * QT * P]
        w_vg = mask[:].rearrange("p h c -> p (h c)")[:, 2 * QT * P:2 * QT * P + 2 * VB]

        s_ps = pb("s", [P, S_RING, 2, 512])
        r_ps = pb("r", [P, TB * VB])
        a_ps = pb("a", [P, 512])
        t_ps = pb("t", [P, 512])
        p_ps = pb("p", [P, 2, SEQ])

        loaded, loaded_mask = sem("loaded"), sem("loaded_mask")
        split_hi, split_lo, preset = sem("split_hi"), sem("split_lo"), sem("preset")
        stats_step, var_eps, rstd_done, xn_done = sem("stats_step"), sem("var_eps"), sem("rstd_done"), sem("xn_done")
        bias_added = sem("bias_added")
        xn_turned, x_hi_done, x_lo_done = sem("xn_turned"), sem("x_hi_done"), sem("x_lo_done")
        projected, f_done, qk_done, vg_done = sem("projected"), sem("f_done"), sem("qk_done"), sem("vg_done")
        scored, mask_done, mixed = sem("scored"), sem("mask_done"), sem("mixed")
        abs_done, summed = sem("abs_done"), sem("summed")
        sums_taken, sums_turned = sem("sums_taken"), sem("sums_turned")
        r_evicted, r_back, r_taken, square_done = sem("r_evicted"), sem("r_back"), sem("r_taken"), sem("square_done")
        norm_step, root_done, r_gated, norm_applied = sem("norm_step"), sem("root_done"), sem("r_gated"), sem("norm_applied")
        gated_turned, gated_t_done, out_done, x_updated = sem("gated_turned"), sem("gated_t_done"), sem("out_done"), sem("x_updated")
        STATS, NORM = 2 * TB, 5
        VG_ITEMS = TB
        ITEMS = QT + VG_ITEMS
        block = ctx.enter_context(nc.Block())

        def first(b):
            return isinstance(b, int) and b == 0

        def last_use(p, ring):
            return p - ring if p >= ring else max(q for q in range(PAIRS) if q % ring == p) - PAIRS

        @block.sync
        def _(sp):
            for dst, src in ((w_qk, m["w_qk_dram"]), (w_vg, m["w_vg_dram"]), (wo[:], m["w_o_dram"]), (bqk[:], m["b_qk_dram"]),
                             (bvg[:], m["b_vg_dram"].partition_broadcast(P)),
                             (bo[:], m["b_o_dram"].partition_broadcast(P))):
                sp.dma_start(dst, src).then_inc(loaded, 16)
            sp.wait_ge(split_lo, 2)
            sp.dma_start(mask[:], m["mask_dram"]).then_inc(loaded_mask, 16)

        @block.tensor
        def _(pe):
            def turn(b):
                pe.wait_ge(xn_done, TB * (b + 1))
                if not isinstance(b, int) or b > 2:
                    pe.wait_ge(norm_step, NORM * (b - 3) + 1)
                for j in range(TB):
                    last = pe.transpose(t_ps[:, j * P:(j + 1) * P], xn[:, j, :], ident)
                last.then_inc(xn_turned, 1)

            def project_qk(b, g):
                if g == 0:
                    pe.wait_ge(x_lo_done, b + 1)
                if not first(b) or g:
                    wait_bank(b, g)
                for k in range(2):
                    cols = slice((2 * g + k) * P, (2 * g + k + 1) * P)
                    pe.matmul(p_ps[:, k, :], wqk_hi[:, cols], x_hi[:], start=True, stop=False)
                    pe.matmul(p_ps[:, k, :], wqk_hi[:, cols], x_lo[:], start=False, stop=False)
                    last = pe.matmul(p_ps[:, k, :], wqk_lo[:, cols], x_hi[:], start=False, stop=True)
                last.then_inc(projected, 1)

            def project_vg(b, j):
                wait_bank(b, QT + j)
                out = p_ps[:].rearrange("p a b -> p (a b)")
                hi, lo = x_hi[:, j * P:(j + 1) * P], x_lo[:, j * P:(j + 1) * P]
                pe.matmul(out, hi, wvg_hi[:], start=True, stop=False)
                pe.matmul(out, hi, wvg_lo[:], start=False, stop=False)
                pe.matmul(out, lo, wvg_hi[:], start=False, stop=True).then_inc(projected, 1)

            def wait_bank(b, item):
                if item == 0:
                    pe.wait_ge(vg_done, VG_ITEMS * b)
                elif item <= QT:
                    pe.wait_ge(f_done, 2 * (QT * b + item))
                else:
                    pe.wait_ge(vg_done, VG_ITEMS * b + item - QT)

            def scores(b, par, p):
                pe.wait_ge(qk_done, QT * b + p // 2 + 1)
                if not first(b) or p >= S_RING:
                    pe.wait_ge(mask_done, PAIRS * b + p - S_RING + 1)
                for i in range(2):
                    g, j = (2 * p + i) // 4, (2 * p + i) % 4
                    rows = slice(32 * j, 32 * j + 32)
                    q, k = qk[par][rows, 2 * g, :], qk[par][rows, 2 * g + 1, :]
                    pe.matmul(s_ps[:, p % S_RING, i, 0:SEQ], k[:, P:SEQ], q, start=True, stop=True)
                    last = pe.matmul(s_ps[:, p % S_RING, i, SEQ:2 * SEQ], k[:, 0:P], q, start=True, stop=True)
                last.then_inc(scored, 1)

            def mix(b, par, p):
                pe.wait_ge(mask_done, PAIRS * b + p + 1)
                if p == 0:
                    pe.wait_ge(vg_done, VG_ITEMS * (b + 1))
                    if not first(b):
                        pe.wait_ge(r_evicted, b)
                rows, base = slice(32 * (p % 4), 32 * (p % 4) + 32), p // 4 * SEQ
                for i in range(2):
                    v0, v1 = (v[par][:, j, p, i:i + 2, :].rearrange("p a d -> p (a d)") for j in range(TB))
                    src = masked[p % M_RING]
                    pe.matmul(r_ps[rows, base:base + SEQ], v0, src[:, i, P:3 * P], start=(i == 0), stop=False)
                    last = pe.matmul(r_ps[rows, base + P:base + SEQ], v1, src[:, i, 0:P], start=False, stop=(i == 1))
                last.then_inc(mixed, 1)

            def add_up(b, p):
                pe.wait_ge(abs_done, PAIRS * b + p + 1)
                if p == 0 and not first(b):
                    pe.wait_ge(sums_taken, b)
                for i in range(2):
                    h = 2 * p + i
                    rows, r = slice(32 * (h % 4), 32 * (h % 4) + 32), h // 4
                    one, src = pick[:, HEADS // 4 - 1 - r:HEADS // 4 - 1 - r + 32], absed[p % A_RING]
                    pe.matmul(a_ps[rows, 0:SEQ], one, src[:, i, P:CAUSAL], start=(r == 0), stop=False)
                    last = pe.matmul(a_ps[rows, P:SEQ], one, src[:, i, 0:P], start=False, stop=(r == HEADS // 4 - 1))
                last.then_inc(summed, 1)

            def turn_r(b):
                pe.wait_ge(r_evicted, b + 1)
                if first(b):
                    pe.wait_ge(x_lo_done, 3)
                else:
                    pe.wait_ge(x_updated, b)
                for j in range(TB):
                    for k in range(VB // P):
                        last = pe.transpose(t_ps[:, j * VB + k * P:j * VB + (k + 1) * P],
                                            r_turned[:, k * SEQ + j * P:k * SEQ + (j + 1) * P], ident)
                last.then_inc(r_back, 1)

            def turn_sums(b):
                pe.wait_ge(sums_taken, b + 1)
                pe.wait_ge(square_done, b + 1)
                for j in range(TB):
                    last = pe.transpose(t_ps[:, j * P:(j + 1) * P], sums[:, j * P:(j + 1) * P], ident)
                last.then_inc(sums_turned, 1)

            def turn_gated(b):
                pe.wait_ge(norm_applied, b + 1)
                if not isinstance(b, int) or b < seqs - 3:
                    pe.wait_ge(x_lo_done, b + 4)
                for j in range(TB):
                    for k in range(VB // P):
                        last = pe.transpose(t_ps[:, k * SEQ + j * P:k * SEQ + (j + 1) * P],
                                            r_sb[:, j * VB + k * P:j * VB + (k + 1) * P], ident)
                last.then_inc(gated_turned, 1)

            def project_out(b):
                pe.wait_ge(gated_t_done, b + 1)
                for j in range(TB):
                    for k in range(VB // P):
                        last = pe.matmul(t_ps[:, j * P:(j + 1) * P], gated_t[:, k * SEQ + j * P:k * SEQ + (j + 1) * P],
                                         wo[:, k, :], start=(k == 0), stop=(k == VB // P - 1))
                last.then_inc(out_done, 1)

            def sequence(b, par, prep=True):
                for p in range(PAIRS):
                    if p:
                        mix(b, par, p - 1)
                    elif not first(b):
                        mix(b - 1, 1 - par, PAIRS - 1)
                    if prep and p == 0:
                        turn(b + 1)
                    if p < PAIRS - 1:
                        scores(b, par, p + 1)
                    elif prep:
                        scores(b + 1, 1 - par, 0)
                    if p >= 2:
                        add_up(b, p - 2)
                    elif not first(b):
                        add_up(b - 1, PAIRS - 2 + p)
                    if not isinstance(b, int) or b > 1:
                        if p == 1:
                            turn_gated(b - 2)
                        if p == 2:
                            project_out(b - 2)
                    if not first(b):
                        if p == 4:
                            turn_r(b - 1)
                        if p == 5:
                            turn_sums(b - 1)
                    if prep:
                        if 0 < p <= QT:
                            project_qk(b + 1, p - 1)
                        elif QT < p <= ITEMS:
                            project_vg(b + 1, p - QT - 1)

            pe.wait_ge(preset, 3)
            pe.wait_ge(split_lo, 2)
            turn(0)
            for g in range(QT):
                project_qk(0, g)
            for j in range(TB):
                project_vg(0, j)
            scores(0, 0, 0)
            sequence(0, 0)
            sequence(1, 1)
            with pe.Fori(1, seqs // 2 - 1) as two:
                sequence(2 * two, 0)
                sequence(2 * two + 1, 1)
            sequence(seqs - 2, 0)
            sequence(seqs - 1, 1, prep=False)
            mix(seqs - 1, 1, PAIRS - 1)
            add_up(seqs - 1, PAIRS - 2)
            add_up(seqs - 1, PAIRS - 1)
            turn_gated(seqs - 2)
            project_out(seqs - 2)
            turn_r(seqs - 1)
            turn_sums(seqs - 1)
            turn_gated(seqs - 1)
            project_out(seqs - 1)

        @block.scalar
        def _(act):
            def take_x(b):
                act.wait_ge(xn_turned, b + 1)
                if not first(b):
                    act.wait_ge(projected, ITEMS * b)
                act.activation(x_hi[:], t_ps[:, 0:SEQ], ACT.Copy).then_inc(x_hi_done, 1)

            def take_qk(b, par, g):
                act.wait_ge(projected, ITEMS * b + g + 1)
                if not isinstance(b, int) or b > 1:
                    act.wait_ge(scored, PAIRS * (b - 1))
                for k in range(2):
                    act.activation(qk[par][:, 2 * g + k, :], p_ps[:, k, :], ACT.Identity,
                                   bias=bqk[:, 2 * g + k:2 * g + k + 1])
                if not first(b) or g >= F_RING:
                    act.wait_ge(qk_done, QT * b + g - F_RING + 1)
                for k in range(2):
                    act.activation(f[g % F_RING][:, k, :], p_ps[:, k, :], ACT.Identity,
                                   bias=bqk[:, 2 * g + k:2 * g + k + 1]).then_inc(f_done, 1)

            def magnitudes(b, p):
                act.wait_ge(mask_done, PAIRS * b + p + 1)
                if not first(b) or p >= A_RING:
                    act.wait_ge(summed, PAIRS * b + last_use(p, A_RING) + 1)
                act.activation(absed[p % A_RING][:], masked[p % M_RING][:], ACT.Abs).then_inc(abs_done, 1)

            def evict_r(b):
                act.wait_ge(mixed, PAIRS * (b + 1))
                if not first(b):
                    act.wait_ge(r_back, b)
                act.activation(r_turned[:], r_ps[:], ACT.Copy).then_inc(r_evicted, 1)

            def take_r(b):
                act.wait_ge(r_back, b + 1)
                if not first(b):
                    act.wait_ge(gated_turned, b)
                act.activation(r_sb[:], t_ps[:], ACT.Copy).then_inc(r_taken, 1)
                if not first(b):
                    act.wait_ge(out_done, b)
                act.activation(square[:], t_ps[:], ACT.Square).then_inc(square_done, 1)

            def take_sums(b):
                act.wait_ge(summed, PAIRS * (b + 1))
                if not first(b):
                    act.wait_ge(sums_turned, b)
                act.activation(sums[:], a_ps[:, 0:SEQ], ACT.Copy).then_inc(sums_taken, 1)

            def take_gated(b):
                act.wait_ge(gated_turned, b + 1)
                act.wait_ge(norm_step, NORM * (b + 1))
                act.activation(gated_t[:], t_ps[:], ACT.Copy).then_inc(gated_t_done, 1)

            def root(b):
                act.wait_ge(norm_step, NORM * b + 4)
                act.activation(ssum[:], ssum[:], ACT.Sqrt).then_inc(root_done, 1)

            def sequence(b, par, prep=True):
                for p in range(PAIRS):
                    if p == 0 and not first(b):
                        evict_r(b - 1)
                    if prep and p == 0:
                        take_x(b + 1)
                    if prep and 2 <= p <= QT + 1:
                        take_qk(b + 1, 1 - par, p - 2)
                    if p == 5 and not first(b):
                        take_r(b - 1)
                    if p == 7 and not first(b):
                        root(b - 1)
                    magnitudes(b, p)
                    if p == 1:
                        if not isinstance(b, int) or b > 1:
                            take_gated(b - 2)
                        if not first(b):
                            take_sums(b - 1)

            act.wait_ge(loaded, 96)
            act.activation(wqk_hi[:], w_qk, ACT.Copy).then_inc(split_hi, 1)
            act.activation(wvg_hi[:], w_vg, ACT.Copy).then_inc(split_hi, 1)
            take_x(0)
            for g in range(QT):
                take_qk(0, 0, g)
            sequence(0, 0)
            sequence(1, 1)
            with act.Fori(1, seqs // 2 - 1) as two:
                sequence(2 * two, 0)
                sequence(2 * two + 1, 1)
            sequence(seqs - 2, 0)
            sequence(seqs - 1, 1, prep=False)
            evict_r(seqs - 1)
            take_gated(seqs - 2)
            take_sums(seqs - 1)
            take_r(seqs - 1)
            root(seqs - 1)
            take_gated(seqs - 1)

        @block.vector
        def _(dve):
            def prep_stats(b):
                if not first(b):
                    dve.wait_ge(rstd_done, b)
                    dve.wait_ge(xn_done, TB * b)
                for j in range(TB):
                    dve.bn_stats(stats[:, j, :], x[:, ds(TB * b + j, 1), :].squeeze(1)).then_inc(stats_step, 1)
                dve.wait_ge(stats_step, STATS * b + TB)
                dve.memset(carrier[:], 0.0)
                for j in range(TB):
                    dve.bn_aggr(mv[:, j, :], stats[:, j, :]).then_inc(stats_step, 1)

            def prep_normalise(b):
                dve.wait_ge(rstd_done, b + 1)
                dve.wait_ge(stats_step, STATS * (b + 1))
                if not first(b):
                    dve.wait_ge(xn_turned, b)
                for j in range(TB):
                    dve.tensor_scalar(xn[:, j, :], x[:, ds(TB * b + j, 1), :].squeeze(1), mv[:, j, 0:1],
                                      rstd[:, j:j + 1], ALU.subtract, ALU.mult).then_inc(xn_done, 1)

            def split_x(b):
                dve.wait_ge(x_hi_done, b + 1)
                dve.tensor_tensor(x_lo[:], t_ps[:, 0:SEQ], x_hi[:].bitcast(F32), ALU.subtract).then_inc(x_lo_done, 1)

            def split_qk(b, par, g):
                dve.wait_ge(f_done, 2 * (QT * b + g + 1))
                for k in range(2):
                    part = qk[par][:, 2 * g + k, :]
                    low = const[:, C_QLOW + k:C_QLOW + k + 1]
                    last = dve.scalar_tensor_tensor(part, part.bitcast(F32), low, f[g % F_RING][:, k, :], ALU.mult, ALU.add)
                last.then_inc(qk_done, 1)

            def take_vg(b, par, j):
                dve.wait_ge(projected, ITEMS * b + QT + j + 1)
                if not first(b) and not (isinstance(b, int) and b < 2):
                    dve.wait_ge(mixed, PAIRS * (b - 1))
                    dve.wait_ge(r_gated, b - 1)
                flat = p_ps[:].rearrange("p a b -> p (a b)")
                pairs = "p (q i d) -> p q i d"
                dve.tensor_tensor(v[par][:, j, :, 0:3:2, :], flat[:, 0:VB].rearrange(pairs, q=PAIRS, i=2),
                                  bvg[:, 0:VB].rearrange(pairs, q=PAIRS, i=2), ALU.add)
                dve.tensor_tensor(gates[par][:, j, :], flat[:, VB:2 * VB], bvg[:, VB:2 * VB], ALU.add)\
                   .then_inc(vg_done, 1)

            def apply_mask(b, p):
                dve.wait_ge(scored, PAIRS * b + p + 1)
                if not first(b) or p >= M_RING:
                    dve.wait_ge(mixed, PAIRS * b + last_use(p, M_RING) + 1)
                    dve.wait_ge(abs_done, PAIRS * b + last_use(p, M_RING) + 1)
                dve.tensor_tensor(masked[p % M_RING][:], s_ps[:, p % S_RING, :, P:4 * P], mask[:, 2 * p:2 * p + 2, :],
                                  ALU.mult).then_inc(mask_done, 1)

            def norm_denominator(b):
                base = NORM * b
                dve.wait_ge(sums_turned, b + 1)
                if not first(b):
                    dve.wait_ge(norm_step, base)
                taken = t_ps[:, 0:SEQ].rearrange("p (j i k) -> p j i k", j=TB, k=32)[:, :, :, 0:HEADS // 4]
                dve.tensor_scalar(denom[:].rearrange("p (j k i) -> p j i k", j=TB, i=4), taken, DENOM_LO, DENOM_HI,
                                  ALU.max, ALU.min).then_inc(norm_step, 1)
                dve.wait_ge(norm_step, base + 1)
                dve.scalar_tensor_tensor(denom[:], denom[:], RMS_EPS, denom[:], ALU.mult, ALU.mult).then_inc(norm_step, 1)

            def norm_power(b):
                base = NORM * b
                dve.wait_ge(norm_step, base + 2)
                dve.wait_ge(square_done, b + 1)
                if not first(b):
                    dve.wait_ge(norm_applied, b)
                dve.tensor_reduce(ssum[:], square[:].rearrange("p (h d) -> p h d", d=VD), AX.X, ALU.add).then_inc(norm_step, 1)
                dve.wait_ge(norm_step, base + 3)
                dve.scalar_tensor_tensor(ssum[:], ssum[:], 1.0 / VD, denom[:], ALU.mult, ALU.add).then_inc(norm_step, 1)

            def norm_scale(b):
                dve.wait_ge(root_done, b + 1)
                dve.reciprocal(ssum[:], ssum[:]).then_inc(norm_step, 1)

            def norm_apply(b):
                wide = r_sb[:].rearrange("p (h d) -> p h d", d=VD)
                dve.wait_ge(r_gated, b + 1)
                dve.wait_ge(norm_step, NORM * (b + 1))
                dve.tensor_tensor(wide, wide, ssum[:].unsqueeze(2).to_broadcast([P, TB * HEADS, VD]), ALU.mult)\
                   .then_inc(norm_applied, 1)

            def update(b):
                dve.wait_ge(out_done, b + 1)
                dve.wait_ge(bias_added, b + 1)
                rows = x[:, ds(TB * b, TB), :].rearrange("p j c -> p (j c)")
                dve.tensor_tensor(rows, t_ps[:, 0:SEQ], rows, ALU.add).then_inc(x_updated, 1)

            def sequence(b, par, prep=True):
                for p in range(PAIRS):
                    if prep and p == 6:
                        take_vg(b + 1, 1 - par, 0)
                    apply_mask(b, p)
                    if p == 7 and prep and not is_second_last(b):
                        prep_normalise(b + 2)
                    if prep and p == 7:
                        take_vg(b + 1, 1 - par, 1)
                    if prep:
                        if p == 0:
                            split_x(b + 1)
                        elif 2 <= p <= QT + 1:
                            split_qk(b + 1, 1 - par, p - 2)
                        if p == 5 and not is_second_last(b):
                            prep_stats(b + 2)
                    if not isinstance(b, int) or b > 1:
                        if p == 0:
                            norm_apply(b - 2)
                        if p == 3:
                            update(b - 2)
                    if not first(b):
                        if p == 6:
                            norm_denominator(b - 1)
                            norm_power(b - 1)
                        if p == 7:
                            norm_scale(b - 1)

            def is_second_last(b):
                return isinstance(b, int) and b == seqs - 2

            dve.memset(half_neg[:], -0.5)
            dve.memset(eps[:], LN_EPS).then_inc(preset, 1)
            for i in range(2):
                dve.memset(v[i][:, :, :, 1, :], 0.0)
            dve.memset(pick[:], 0.0).then_inc(preset, 1)
            dve.wait_ge(preset, 2)
            dve.memset(pick[:, HEADS // 4 - 1:HEADS // 4], 1.0).then_inc(preset, 1)
            prep_stats(0)
            prep_normalise(0)
            for k, (lo, src, hi) in enumerate(((wqk_lo, w_qk, wqk_hi), (wvg_lo, w_vg, wvg_hi))):
                dve.wait_ge(split_hi, k + 1)
                dve.tensor_tensor(lo[:], src, hi[:].bitcast(F32), ALU.subtract).then_inc(split_lo, 1)
            dve.wait_ge(split_lo, 2)
            split_x(0)
            for g in range(QT):
                split_qk(0, 0, g)
            for j in range(TB):
                take_vg(0, 0, j)
            prep_stats(1)
            prep_normalise(1)
            dve.wait_ge(loaded_mask, 16)
            sequence(0, 0)
            sequence(1, 1)
            with dve.Fori(1, seqs // 2 - 1) as two:
                sequence(2 * two, 0)
                sequence(2 * two + 1, 1)
            sequence(seqs - 2, 0)
            sequence(seqs - 1, 1, prep=False)
            norm_apply(seqs - 2)
            update(seqs - 2)
            norm_denominator(seqs - 1)
            norm_power(seqs - 1)
            norm_scale(seqs - 1)
            norm_apply(seqs - 1)
            update(seqs - 1)

        @block.gpsimd
        def _(pool):
            def prep_rstd(b):
                pool.wait_ge(stats_step, STATS * (b + 1))
                if not first(b):
                    pool.wait_ge(xn_done, TB * b)
                pool.tensor_tensor(veps[:], mv[:, :, 1], eps[:], ALU.add).then_inc(var_eps, 1)
                pool.wait_ge(var_eps, b + 1)
                pool.tensor_tensor(rstd[:], veps[:], half_neg[:], ALU.pow).then_inc(rstd_done, 1)

            def add_bias(b):
                pool.wait_ge(xn_done, TB * (b + 1))
                rows = x[:, ds(TB * b, TB), :]
                pool.tensor_tensor(rows, rows, bo[:].unsqueeze(1).to_broadcast([P, TB, P]), ALU.add).then_inc(bias_added, 1)

            def apply_gates(b, par):
                pool.wait_ge(r_taken, b + 1)
                flat = r_sb[:].rearrange("p (j c) -> p j c", j=TB)
                pool.tensor_tensor(flat, flat, gates[par][:], ALU.mult).then_inc(r_gated, 1)

            def sequence(b, par, prep=True):
                if prep:
                    add_bias(b + 1)
                if not first(b):
                    apply_gates(b - 1, 1 - par)
                if prep and not (isinstance(b, int) and b == seqs - 2):
                    prep_rstd(b + 2)

            pool.wait_ge(preset, 3)
            prep_rstd(0)
            pool.wait_ge(loaded, 96)
            add_bias(0)
            prep_rstd(1)
            sequence(0, 0)
            sequence(1, 1)
            with pool.Fori(1, seqs // 2 - 1) as two:
                sequence(2 * two, 0)
                sequence(2 * two + 1, 1)
            sequence(seqs - 2, 0)
            sequence(seqs - 1, 1, prep=False)
            apply_gates(seqs - 1, 1)


def build(nc, x, const, mask, w_qk, b_qk, w_vg, b_vg, w_o, b_o, wfc_s, wproj_s, wr, wfc, wproj, biases,
          x_slots, y_slots, out):
    tokens = x.shape[0]
    ctx = ExitStack()
    with ctx:
        def sb(n, shape, dt=F32):
            return ctx.enter_context(nc.sbuf_tensor(n, shape, dt))

        m = {
            "tokens": tokens,
            "scattered": [ctx.enter_context(nc.semaphore(f"scattered{i}")) for i in range(2)],
            "gathered_half": ctx.enter_context(nc.semaphore("gathered_half")),
            "gathered": [ctx.enter_context(nc.semaphore(f"gathered{i}")) for i in range(G_RING)],
            "x": sb("x", [P, tokens // P, P]),
            "w_hi": sb("w_hi", [P, EX, 2 * HID], F32R),
            "w_lo": sb("w_lo", [P, EX, 2 * HID], F32R),
            "const": sb("const", [P, C_END]),
            "x_dram": x.rearrange("(n p) c -> p n c", p=P),
            "out_dram": out.rearrange("(n p) c -> p n c", p=P),
            "const_dram": const, "wr_dram": wr, "bias_dram": biases,
            "w_dram": [(wfc_s, wproj_s.rearrange("(c p) n -> p c n", p=P))]
                      + [(wfc[e], wproj[e].rearrange("(c p) n -> p c n", p=P)) for e in range(NE)],
            "x_slot_rows": x_slots, "x_slots": [a.rearrange("(n p) c -> p n c", p=P) for a in x_slots],
            "y_slot_rows": y_slots, "y_slots": [a.rearrange("(n p) c -> p n c", p=P) for a in y_slots],
            "mask_dram": mask, "w_qk_dram": w_qk, "b_qk_dram": b_qk, "w_vg_dram": w_vg, "b_vg_dram": b_vg,
            "w_o_dram": w_o.rearrange("(k p) n -> p k n", p=P), "b_o_dram": b_o,
        }
        ffn_phase(nc, m, "ffn1", load=True, store=False)
        retention_phase(nc, m)
        ffn_phase(nc, m, "ffn2", load=False, store=True)


def decay_mask():
    gamma = np.log(1.0 - 2.0 ** (-5.0 - np.arange(HEADS)))
    at = np.arange(SEQ)
    diff = at[:, None] - at[None, :]
    decay = np.where(diff >= 0, np.exp(gamma[:, None, None] * np.maximum(diff, 0)), 0.0)
    full = (decay / np.sqrt(decay.sum(-1, keepdims=True))).transpose(2, 0, 1)
    blocks = (full[P:, :, P:], full[:P, :, :P], full[:P, :, P:])
    return np.ascontiguousarray(np.concatenate(blocks, axis=2)).astype(np.float32)


def constants():
    c = np.zeros((P, C_END), np.float32)
    c[:, C_ID:C_ID + P] = np.eye(P)
    c[:, C_BEFORE:C_BEFORE + P] = np.triu(np.ones((P, P)), 1)
    c[:, C_IOTA:C_IOTA + NE] = np.arange(NE) - NE
    c[:, C_LOWER:C_LOWER + NE * NE] = np.tril(np.ones((NE, NE)), -1).reshape(-1)
    c[:, C_FULL:C_FULL + MOST] = JOB * np.arange(MOST)
    c[:, C_JOB:C_JOB + HALF_JOBS] = np.arange(HALF_JOBS)
    half = np.arange(P) // (P // 2)
    c[:, C_SAME:C_SAME + P] = np.where(half[:, None] == half, c[:, C_BEFORE:C_BEFORE + P], 0)
    c[:, C_SAME + P:C_END] = half[:, None]
    copy = np.arange(P) // KD % 4
    c[:, C_QLOW] = np.where(copy >= 2, -1.0, 0.0)
    c[:, C_KLOW] = np.where(copy % 2 == 1, -1.0, 0.0)
    return c


def kernel(L0_attn_x, L0_attn_W_qk, L0_attn_b_qk, L0_attn_W_v, L0_attn_b_v, L0_attn_W_g, L0_attn_b_g,
           L0_attn_W_o, L0_attn_b_o, L0_ffn_Wfc_s, L0_ffn_bfc_s, L0_ffn_Wproj_s, L0_ffn_bproj_s, L0_ffn_Wr,
           L0_ffn_Wfc, L0_ffn_bfc, L0_ffn_Wproj, L0_ffn_bproj):
    import concourse.bacc as bacc
    from concourse.bass_utils import run_bass_kernel_spmd

    g, kind, j, copy, d = np.ix_(range(QT), range(2), range(4), range(4), range(KD))
    spread = (kind * P + (4 * g + j) * KD + d + 0 * copy).reshape(-1)
    shape = np.shape(L0_attn_x)
    arrays = {
        "x": np.reshape(L0_attn_x, (-1, P)),
        "const": constants(),
        "mask": decay_mask(),
        "w_qk": np.asarray(L0_attn_W_qk)[:, spread],
        "b_qk": np.asarray(L0_attn_b_qk)[spread].reshape(2 * QT, P).T,
        "w_vg": np.concatenate([L0_attn_W_v, L0_attn_W_g], axis=1),
        "b_vg": np.concatenate([L0_attn_b_v, L0_attn_b_g]),
        "w_o": L0_attn_W_o,
        "b_o": L0_attn_b_o,
        "wfc_s": L0_ffn_Wfc_s,
        "wproj_s": L0_ffn_Wproj_s,
        "wr": L0_ffn_Wr,
        "wfc": L0_ffn_Wfc,
        "wproj": L0_ffn_Wproj,
        "biases": np.concatenate([np.concatenate([np.reshape(L0_ffn_bfc_s, (1, CH, P)), np.reshape(L0_ffn_bfc, (NE, CH, P))]),
                                  np.concatenate([np.reshape(L0_ffn_bproj_s, (1, 1, P)), np.reshape(L0_ffn_bproj, (NE, 1, P))])],
                                 axis=1).transpose(2, 0, 1),
    }
    nc = bacc.Bacc("TRN2", target_bir_lowering=False, num_devices=1)
    feeds, args = {}, []
    for name, a in arrays.items():
        a = np.ascontiguousarray(a)
        feeds[f"in_{name}"] = a
        args.append(nc.dram_tensor(f"in_{name}", a.shape, mybir.dt.from_np(a.dtype), kind="ExternalInput").ap())
    for name in ("x_slots", "y_slots"):
        args.append([nc.dram_tensor(f"{name}{half}", (HALF_JOBS * JOB, P), F32).ap() for half in range(2)])
    args.append(nc.dram_tensor("out", feeds["in_x"].shape, F32, kind="ExternalOutput").ap())
    build(nc, *args)
    result = run_bass_kernel_spmd(nc, [feeds], core_ids=[0])
    return np.reshape(result.results[0]["out"], shape)
```
